# Optimizing a Trainium2 kernel written in Bass

```python
import numpy as np
import jax
import jax.numpy as jnp

def _softmax(x, axis=-1):
    return jax.nn.softmax(x, axis=axis)

def _gelu(x):
    return jax.nn.gelu(x, approximate=True)

def _silu(x):
    return jax.nn.silu(x)

def _sigmoid(x):
    return jax.nn.sigmoid(x)

def _layernorm(x, axis=-1, eps=1e-05):
    m = jnp.mean(x, axis=axis, keepdims=True)
    v = jnp.var(x, axis=axis, keepdims=True)
    return (x - m) / jnp.sqrt(v + eps)

def _scatter_add(tgt, idx, src, axis=0):
    return tgt.at[idx].add(src)

def _segment_sum(src, seg, n):
    return jax.ops.segment_sum(src, seg, n)
kernel_name = 'mk_lm_tower_d1_tok_ids2048_r4_32d841'

def setup_inputs(seed: int=0):
    np.random.seed(seed)
    _w = jnp.asarray

    def _rec_inputs():
        import jax
        import jax.numpy as jnp
        _rk = jax.random.key(seed)
        x = jax.random.randint(jax.random.fold_in(_rk, 1), (2, 1024), 0, 8000, jnp.int32)
        return x
    x = _rec_inputs()

    def _L0_tok_setup():
        import jax, jax.numpy as jnp
        import numpy as np
        VOCAB = 8000
        DIM = 512
        RANK = 16
        ALPHA = 32
        SCALING = ALPHA / RANK
        key = jax.random.key(seed)
        k1, k2, k3, k4 = jax.random.split(key, 4)
        x = jax.random.randint(k1, (4, 2048), 0, VOCAB, dtype=jnp.int64 if jax.config.jax_enable_x64 else jnp.int32)
        weight = jax.random.normal(k2, (VOCAB, DIM), dtype=jnp.float32)
        lora_A = jax.random.normal(k3, (VOCAB, RANK), dtype=jnp.float32)
        lora_B = jax.random.normal(k4, (RANK, DIM), dtype=jnp.float32)
        return {'x': x, 'weight': weight, 'lora_A': lora_A, 'lora_B': lora_B}
    _L0_tok_all = _L0_tok_setup()
    _L0_tok_in = {k: v for k, v in _L0_tok_all.items() if k in ('weight', 'lora_A', 'lora_B')}
    del _L0_tok_all

    def _L0_attn_setup():
        import jax, jax.numpy as jnp
        import numpy as np
        EMBED_DIM = 512
        NUM_HEADS = 16
        HEAD_DIM = EMBED_DIM // NUM_HEADS
        key = jax.random.key(seed)
        k_x, k_qkv, k_out = jax.random.split(key, 3)
        x = jax.random.normal(k_x, (4, 512, EMBED_DIM), dtype=jnp.float32)
        scale = 1.0 / np.sqrt(EMBED_DIM)
        W_qkv = jax.random.uniform(k_qkv, (3 * EMBED_DIM, EMBED_DIM), dtype=jnp.float32, minval=-scale, maxval=scale)
        W_out = jax.random.uniform(k_out, (EMBED_DIM, EMBED_DIM), dtype=jnp.float32, minval=-scale, maxval=scale)
        return {'x': x, 'W_qkv': W_qkv, 'W_out': W_out}
    _L0_attn_all = _L0_attn_setup()
    _L0_attn_in = {k: v for k, v in _L0_attn_all.items() if k in ('W_qkv', 'W_out')}
    del _L0_attn_all

    def _L0_ffn_setup():
        import jax, jax.numpy as jnp
        import numpy as np
        FP8_MAX = 448.0
        GLOBAL_DIV = 448.0 * 6.0

        def _fp8(x):
            return x.astype(jnp.float8_e4m3fn).astype(jnp.float32)

        def _reorder_quantize_x(x, idx):
            scale = jnp.max(jnp.abs(x)) / GLOBAL_DIV
            xr = (x / scale)[:, idx]
            scale_x = jnp.max(jnp.abs(xr), axis=1, keepdims=True) / FP8_MAX
            qx = _fp8(xr / scale_x)
            return (qx, scale_x, scale)

        def _qlinear(qx, scale_x, scale, W, idx, out_idx=None):
            Wr = W[:, idx]
            w_scale = jnp.max(jnp.abs(Wr), axis=1, keepdims=True) / FP8_MAX
            qw = _fp8(Wr / w_scale)
            y = qx * scale_x @ (qw * w_scale).T * scale
            if out_idx is not None:
                y = y[:, out_idx]
            return y
        key = jax.random.key(seed)
        ks = jax.random.split(key, 6)
        B, S, H, I = (2, 256, 512, 1408)
        return {'x': jax.random.normal(ks[0], (B, S, H), jnp.float32), 'w_gate': jax.random.normal(ks[1], (I, H), jnp.float32) * 0.02, 'w_up': jax.random.normal(ks[2], (I, H), jnp.float32) * 0.02, 'w_down': jax.random.normal(ks[3], (H, I), jnp.float32) * 0.02, 'up_reorder_index': jax.random.permutation(ks[4], jnp.arange(H, dtype=jnp.int64)), 'down_reorder_index': jax.random.permutation(ks[5], jnp.arange(I, dtype=jnp.int64))}
    _L0_ffn_all = _L0_ffn_setup()
    _L0_ffn_in = {k: v for k, v in _L0_ffn_all.items() if k in ('w_gate', 'w_up', 'w_down', 'up_reorder_index', 'down_reorder_index')}
    del _L0_ffn_all
    return {'x': x, 'L0_tok_weight': _L0_tok_in['weight'], 'L0_tok_lora_A': _L0_tok_in['lora_A'], 'L0_tok_lora_B': _L0_tok_in['lora_B'], 'L0_attn_W_qkv': _L0_attn_in['W_qkv'], 'L0_attn_W_out': _L0_attn_in['W_out'], 'L0_ffn_w_gate': _L0_ffn_in['w_gate'], 'L0_ffn_w_up': _L0_ffn_in['w_up'], 'L0_ffn_w_down': _L0_ffn_in['w_down'], 'L0_ffn_up_reorder_index': _L0_ffn_in['up_reorder_index'], 'L0_ffn_down_reorder_index': _L0_ffn_in['down_reorder_index']}

def reference(x, L0_tok_weight, L0_tok_lora_A, L0_tok_lora_B, L0_attn_W_qkv, L0_attn_W_out, L0_ffn_w_gate, L0_ffn_w_up, L0_ffn_w_down, L0_ffn_up_reorder_index, L0_ffn_down_reorder_index):
    import jax
    import jax.numpy as jnp

    def _L0_tok_ref(x, weight, lora_A, lora_B):
        import jax, jax.numpy as jnp
        import numpy as np
        VOCAB = 8000
        DIM = 512
        RANK = 16
        ALPHA = 32
        SCALING = ALPHA / RANK
        base = weight[x]
        lora = jnp.einsum('bsr,rd->bsd', lora_A[x], lora_B)
        return base + SCALING * lora

    def _L0_attn_ref(x, W_qkv, W_out):
        import jax, jax.numpy as jnp
        import numpy as np
        EMBED_DIM = 512
        NUM_HEADS = 16
        HEAD_DIM = EMBED_DIM // NUM_HEADS
        B, T, C = x.shape
        H, D = (NUM_HEADS, HEAD_DIM)
        qkv = jnp.einsum('btc,fc->btf', x, W_qkv)
        q, k, v = jnp.split(qkv, 3, axis=-1)
        q = q.reshape(B, T, H, D).transpose(0, 2, 1, 3)
        k = k.reshape(B, T, H, D).transpose(0, 2, 1, 3)
        v = v.reshape(B, T, H, D).transpose(0, 2, 1, 3)
        att = jnp.einsum('bhqd,bhkd->bhqk', q, k) / jnp.sqrt(jnp.float32(D))
        causal = jnp.tril(jnp.ones((T, T), dtype=bool))
        att = jnp.where(causal[None, None], att, -jnp.inf)
        att = jax.nn.softmax(att, axis=-1)
        out = jnp.einsum('bhqk,bhkd->bhqd', att, v)
        out = out.transpose(0, 2, 1, 3).reshape(B, T, C)
        return jnp.einsum('btc,oc->bto', out, W_out)

    def _L0_ffn_ref(x, w_gate, w_up, w_down, up_reorder_index, down_reorder_index):
        import jax, jax.numpy as jnp
        import numpy as np
        FP8_MAX = 448.0
        GLOBAL_DIV = 448.0 * 6.0

        def _fp8(x):
            return x.astype(jnp.float8_e4m3fn).astype(jnp.float32)

        def _reorder_quantize_x(x, idx):
            scale = jnp.max(jnp.abs(x)) / GLOBAL_DIV
            xr = (x / scale)[:, idx]
            scale_x = jnp.max(jnp.abs(xr), axis=1, keepdims=True) / FP8_MAX
            qx = _fp8(xr / scale_x)
            return (qx, scale_x, scale)

        def _qlinear(qx, scale_x, scale, W, idx, out_idx=None):
            Wr = W[:, idx]
            w_scale = jnp.max(jnp.abs(Wr), axis=1, keepdims=True) / FP8_MAX
            qw = _fp8(Wr / w_scale)
            y = qx * scale_x @ (qw * w_scale).T * scale
            if out_idx is not None:
                y = y[:, out_idx]
            return y
        B, S, H = x.shape
        xf = x.reshape(B * S, H)
        qx, sx, sc = _reorder_quantize_x(xf, up_reorder_index)
        g = _qlinear(qx, sx, sc, w_gate, up_reorder_index, out_idx=down_reorder_index)
        u = _qlinear(qx, sx, sc, w_up, up_reorder_index, out_idx=down_reorder_index)
        t = jax.nn.silu(g) * u
        qt, st, sct = _reorder_quantize_x(t, down_reorder_index)
        y = _qlinear(qt, st, sct, w_down, down_reorder_index)
        return y.reshape(B, S, H)
    h = _L0_tok_ref(x, L0_tok_weight, L0_tok_lora_A, L0_tok_lora_B)
    h = h + _L0_attn_ref(_layernorm(h, axis=-1), L0_attn_W_qkv, L0_attn_W_out)
    h = h + _L0_ffn_ref(_layernorm(h, axis=-1), L0_ffn_w_gate, L0_ffn_w_up, L0_ffn_w_down, L0_ffn_up_reorder_index, L0_ffn_down_reorder_index)
    return h

_drawn_inputs = setup_inputs


def setup_inputs(seed=0):
    import zlib

    import numpy as np

    out = dict(_drawn_inputs(seed))
    spreads = {}
    factors = {'L0_attn_W_qkv': 8.0,
     'L0_attn_W_out': 8.0,
     'L0_ffn_w_gate': 5.696,
     'L0_ffn_w_up': 5.669,
     'L0_ffn_w_down': 5.623}
    for name, (base, spread) in spreads.items():
        noise = np.random.default_rng([zlib.crc32(name.encode()), seed]).standard_normal(out[name].shape)
        drawn = base * np.exp(spread * noise) if base else spread * noise
        out[name] = jnp.asarray(drawn.astype(out[name].dtype))
    for name, factor in factors.items():
        out[name] = (out[name] * factor).astype(out[name].dtype)
    return out
```

```python
from contextlib import ExitStack

import concourse.bass as bass
from concourse import mybir

ds = bass.ds
ALU = mybir.AluOpType
ACT = mybir.ActivationFunctionType
AX_X = mybir.AxisListType.X
F32 = mybir.dt.float32
F32R = mybir.dt.float32r
BF16 = mybir.dt.bfloat16
I32 = mybir.dt.int32
U32 = mybir.dt.uint32

P = 128
B, S = 2, 1024
D = 512
KC = D // P
NT = B * S // P
H, HD = 16, 32
GH = P // HD
G = H // GH
RANK = 16
LORA_SCALING = 2.0
I_FF = 1408
NI = I_FF // P
GU = 2 * NI
GC = 352
NGC = I_FF // GC
QT = S // P
C = 512
NC = S // C
EPS = 1e-5
FP8_MAX = 448.0
MASKED = -1.0e30
SM_SCALE = float(HD) ** -0.5
NORMAL_MIN = 2.0 ** -6
SHIFT = 2.0 ** 20


def build(nc, x, tok_w, lora_a, lora_b, w_qkv, w_out, w_gate, w_up, w_down, up_idx, down_idx, out):
    h_dram = nc.dram_tensor("h_scratch", (NT, P, D), F32, kind="Internal").ap()
    wqkvT_dram = nc.dram_tensor("wqkvT_scratch", (3, G, P, 2 * D), F32, kind="Internal").ap()
    woT_dram = nc.dram_tensor("woT_scratch", (P, 2 * KC * D), F32, kind="Internal").ap()
    attnT_dram = nc.dram_tensor("attnT_scratch", (G, P, B * S), F32, kind="Internal").ap()
    wguT_dram = nc.dram_tensor("wguT_scratch", (P, KC * 2 * I_FF), BF16, kind="Internal").ap()
    wdT_dram = nc.dram_tensor("wdT_scratch", (P, NI * D), BF16, kind="Internal").ap()
    srow_dram = nc.dram_tensor("srow_scratch", (P, 2 * I_FF + D), F32, kind="Internal").ap()

    with ExitStack() as top:
        identf = top.enter_context(nc.sbuf_tensor("identf", [P, P], F32))
        identb = top.enter_context(nc.sbuf_tensor("identb", [P, P], BF16))
        onesf = top.enter_context(nc.sbuf_tensor("onesf", [P, P], F32))
        with ExitStack() as ctx:
            ffn_weights(nc, ctx, identf, identb, onesf, w_gate, w_up, w_down, down_idx, wguT_dram,
                        wdT_dram, srow_dram)
        with ExitStack() as mid:
            xT = mid.enter_context(nc.sbuf_tensor("xT", [P, 2, KC, B * S], F32R))
            with ExitStack() as ctx:
                tokens(nc, ctx, identf, xT, x, tok_w, lora_a, lora_b, w_qkv, w_out, h_dram,
                       wqkvT_dram, woT_dram)
            with ExitStack() as ctx:
                attend(nc, ctx, identf, identb, onesf, xT, wqkvT_dram, attnT_dram)
        with ExitStack() as ctx:
            feed(nc, ctx, identb, h_dram, attnT_dram, wguT_dram, wdT_dram, srow_dram, woT_dram, out)


def allocators(nc, ctx, block):
    def sb(name, shape, dt=F32):
        return ctx.enter_context(nc.sbuf_tensor(f"{block}_{name}", shape, dt))

    def ps(name, shape, dt=F32):
        return ctx.enter_context(nc.psum_tensor(f"{block}_{name}", shape, dt))

    def sem(name):
        return ctx.enter_context(nc.semaphore(f"{block}_{name}"))

    return sb, ps, sem


def later(n, k):
    return not isinstance(n, int) or n >= k


def ffn_weights(nc, ctx, identf, identb, onesf, w_gate, w_up, w_down, down_idx, wguT_dram,
                wdT_dram, srow_dram):
    sb, ps, sem = allocators(nc, ctx, "ffnw")
    NF = GU + KC
    didx = sb("didx", [P, NI], I32)
    gu_rows = sb("gu_rows", [P, GU, D])
    down_rows = sb("down_rows", [P, KC, I_FF])
    scaled = sb("scaled", [P, 2, I_FF])
    magic = sb("magic", [P, 2, I_FF], U32)
    rounded = sb("rounded", [P, 2, I_FF], BF16)
    row_max = sb("row_max", [P, 2])
    row_scale = sb("row_scale", [P, 2])
    row_rscale = sb("row_rscale", [P, 2])
    diag = sb("diag", [P, 2, P])
    wguT = sb("wguT", [P, KC, 2 * I_FF], BF16)
    wdT = sb("wdT", [P, NI, D], BF16)
    srow = sb("srow", [P, 2 * I_FF + D])
    turned = [ps(f"turned{u}", [P, 2048], BF16) for u in range(2)]
    spread = [ps(f"spread{u}", [P, P]) for u in range(2)]

    idx_in = sem("idx_in")
    gu_in = [sem(f"gu_in{n}") for n in range(2)]
    down_in = sem("down_in")
    ident_made = sem("ident_made")
    dve_step = sem("dve_step")
    scale_made = sem("scale_made")
    scaled_made = sem("scaled_made")
    magic_made = sem("magic_made")
    sum_made = sem("sum_made")
    rounded_made = sem("rounded_made")
    diag_made = sem("diag_made")
    turned_made = sem("turned_made")
    spread_made = sem("spread_made")
    turned_used = sem("turned_used")
    spread_used = sem("spread_used")
    stored = sem("stored")

    block = ctx.enter_context(nc.Block())

    def rows(n, u):
        if isinstance(n, int) and n >= GU:
            return down_rows[:, n - GU, :], I_FF
        return gu_rows[:, ds(n, 1), :].rearrange("p a n -> p (a n)"), D

    @block.sync
    def _(sp):
        sp.dma_start(didx[:, :], down_idx.rearrange("(t p) -> p t", p=P), allow_slow_non_contiguous=True).then_inc(idx_in, 16)
        sp.dma_start(down_rows[:, :, :], w_down.rearrange("(t p) n -> p t n", p=P)).then_inc(down_in, 16)
        sp.wait_ge(turned_used, NF)
        sp.dma_start(wguT_dram[:, :], wguT[:, :, :].rearrange("p k n -> p (k n)")).then_inc(stored, 16)
        sp.dma_start(wdT_dram[:, :], wdT[:, :, :].rearrange("p k n -> p (k n)")).then_inc(stored, 16)
        sp.wait_ge(spread_used, NF)
        sp.dma_start(srow_dram[:, :], srow[:, :]).then_inc(stored, 16)
        sp.wait_ge(stored, 48)

    @block.gpsimd
    def _(pool):
        pool.memset(identf[:, :], 0.0).then_inc(ident_made, 1)
        pool.memset(onesf[:, :], 1.0).then_inc(ident_made, 1)
        pool.wait_ge(ident_made, 2)
        pool.affine_select(out=identf[:, :], in_=identf[:, :], compare_op=ALU.not_equal, fill=1.0,
                           base=0, pattern=[[-1, P]], channel_multiplier=1).then_inc(ident_made, 1)
        pool.wait_ge(ident_made, 3)
        pool.tensor_copy(identb[:, :], identf[:, :]).then_inc(ident_made, 1)
        pool.wait_ge(idx_in, 16)
        for n in range(GU):
            source, r = (w_gate, n) if n < NI else (w_up, n - NI)
            pool.indirect_dma_start(
                out=gu_rows[:, n, :], out_offset=None, in_=source,
                in_offset=bass.IndirectOffsetOnAxis(ap=didx[:, r:r + 1], axis=0),
            ).then_inc(gu_in[n // NI], 16)

        def round_tile(n, u):
            _, N = rows(n, u)
            pool.wait_ge(magic_made, n + 1)
            pool.tensor_tensor(scaled[:, u, 0:N], scaled[:, u, 0:N], magic[:, u, 0:N].bitcast(F32),
                               ALU.add).then_inc(sum_made, 1)
            pool.wait_ge(sum_made, n + 1)
            if later(n, 2):
                pool.wait_ge(turned_made, n - 1)
            pool.tensor_tensor(rounded[:, u, 0:N], scaled[:, u, 0:N],
                               magic[:, u, 0:N].bitcast(F32), ALU.subtract).then_inc(rounded_made, 1)

        for n in range(2):
            round_tile(n, n)
        with pool.Fori(1, GU // 2) as t:
            for u in range(2):
                round_tile(t * 2 + u, u)
        for n in range(GU, NF):
            round_tile(n, n % 2)

    @block.vector
    def _(dve):
        def scale_tile(n, u):
            src, N = rows(n, u)
            k = n * 3
            dve.tensor_reduce(row_max[:, u:u + 1], src, AX_X, ALU.max,
                              apply_absolute_value=True).then_inc(dve_step, 1)
            dve.wait_ge(dve_step, k + 1)
            dve.tensor_scalar(row_scale[:, u:u + 1], row_max[:, u:u + 1], 1.0 / FP8_MAX, None,
                              ALU.mult).then_inc(dve_step, 1)
            dve.wait_ge(dve_step, k + 2)
            dve.reciprocal(row_rscale[:, u:u + 1], row_scale[:, u:u + 1]).then_inc(dve_step, 1)
            dve.wait_ge(dve_step, k + 3)
            if later(n, 2):
                dve.wait_ge(spread_made, n - 1)
            dve.tensor_scalar(diag[:, u, :], identf[:, :], row_scale[:, u:u + 1], None,
                              ALU.mult).then_inc(scale_made, 1)

        def magic_tile(n, u):
            _, N = rows(n, u)
            dve.wait_ge(scaled_made, n + 1)
            if later(n, 2):
                dve.wait_ge(rounded_made, n - 1)
            dve.tensor_scalar(magic[:, u, 0:N], scaled[:, u, 0:N].bitcast(U32), 0x7F800000, None,
                              ALU.bitwise_and).then_inc(diag_made, 1)
            dve.wait_ge(diag_made, n + 1)
            dve.tensor_scalar(magic[:, u, 0:N].bitcast(F32), magic[:, u, 0:N].bitcast(F32),
                              NORMAL_MIN, 1.5 * SHIFT, ALU.max, ALU.mult).then_inc(magic_made, 1)

        dve.wait_ge(ident_made, 4)
        dve.wait_ge(gu_in[0], 16 * NI)
        scale_tile(0, 0)
        scale_tile(1, 1)
        magic_tile(0, 0)
        dve.wait_ge(gu_in[1], 16 * NI)
        with dve.Fori(1, GU // 2) as t:
            scale_tile(t * 2, 0)
            magic_tile(t * 2 - 1, 1)
            scale_tile(t * 2 + 1, 1)
            magic_tile(t * 2, 0)
        dve.wait_ge(down_in, 16)
        for n in range(GU, NF):
            scale_tile(n, n % 2)
            magic_tile(n - 1, 1 - n % 2)
        magic_tile(NF - 1, (NF - 1) % 2)

    @block.scalar
    def _(act):
        def scaled_tile(n, u):
            src, N = rows(n, u)
            act.wait_ge(scale_made, n + 1)
            if later(n, 2):
                act.wait_ge(rounded_made, n - 1)
            act.activation(scaled[:, u, 0:N], src, ACT.Copy, scale=row_rscale[:, u:u + 1]
                           ).then_inc(scaled_made, 1)

        def keep_tile(n, u):
            act.wait_ge(turned_made, n + 1)
            if isinstance(n, int) and n >= GU:
                o = n - GU
                act.activation(wdT[:, :, o * P:(o + 1) * P],
                               turned[u][:, 0:I_FF].rearrange("p (k c) -> p k c", c=P),
                               ACT.Copy).then_inc(turned_used, 1)
            else:
                act.activation(wguT[:, :, ds(n * P, P)],
                               turned[u][:, 0:D].rearrange("p (k c) -> p k c", c=P),
                               ACT.Copy).then_inc(turned_used, 1)
            act.wait_ge(spread_made, n + 1)
            act.activation(srow[:, ds(n * P, P)], spread[u][:, :], ACT.Copy).then_inc(spread_used, 1)

        scaled_tile(0, 0)
        scaled_tile(1, 1)
        keep_tile(0, 0)
        with act.Fori(1, GU // 2) as t:
            scaled_tile(t * 2, 0)
            keep_tile(t * 2 - 1, 1)
            scaled_tile(t * 2 + 1, 1)
            keep_tile(t * 2, 0)
        for n in range(GU, NF):
            scaled_tile(n, n % 2)
            keep_tile(n - 1, 1 - n % 2)
        keep_tile(NF - 1, (NF - 1) % 2)

    @block.tensor
    def _(pe):
        def turn_tile(n, u):
            _, N = rows(n, u)
            pe.wait_ge(scale_made, n + 1)
            if later(n, 2):
                pe.wait_ge(spread_used, n - 1)
            pe.matmul(spread[u][:, :], onesf[:, :], diag[:, u, :], start=True, stop=True
                      ).then_inc(spread_made, 1)
            pe.wait_ge(rounded_made, n + 1)
            for k in range(N // P):
                mm = pe.transpose(turned[u][:, k * P:(k + 1) * P], rounded[:, u, k * P:(k + 1) * P],
                                  identb[:, :])
            mm.then_inc(turned_made, 1)

        pe.wait_ge(ident_made, 4)
        for n in range(2):
            turn_tile(n, n)
        with pe.Fori(1, GU // 2) as t:
            for u in range(2):
                turn_tile(t * 2 + u, u)
        for n in range(GU, NF):
            turn_tile(n, n % 2)


def tokens(nc, ctx, identf, xT, x, tok_w, lora_a, lora_b, w_qkv, w_out, h_dram, wqkvT_dram,
           woT_dram):
    sb, ps, sem = allocators(nc, ctx, "tok")
    tok_ids = sb("tok_ids", [P, NT], I32)
    emb = sb("emb", [P, 2, D])
    lrow = sb("lrow", [P, 2, RANK])
    lrowT = sb("lrowT", [RANK, 2, P])
    lb = sb("lb", [RANK, D])
    hid = sb("hid", [P, 2, D])
    stats = sb("stats", [P, 2, 6])
    mean_var = sb("mean_var", [P, 2, 2])
    var_eps = sb("var_eps", [P, 2])
    rstd = sb("rstd", [P, 2])
    minus_half = sb("minus_half", [P, 1])
    eps = sb("eps", [P, 1])
    xn = sb("xn", [P, 2, D])
    wrows = sb("wrows", [P, 4, G, D])
    wT = sb("wT", [P, 3, G, 2, D], F32R)
    woT = sb("woT", [P, 2, KC, D], F32R)
    turned = [ps(f"turned{u}", [P, D]) for u in range(2)]
    wturned = [ps(f"wturned{u}", [P, D]) for u in range(2)]
    lora = ps("lora", [P, D])
    lturned = ps("lturned", [P, D])

    ids_in = sem("ids_in")
    lb_in = sem("lb_in")
    w_in = [sem(f"w_in{k}") for k in range(4)]
    w_turned = sem("w_turned")
    w_hi = sem("w_hi")
    w_lo = sem("w_lo")
    emb_in = [sem(f"emb_in{u}") for u in range(2)]
    l_turned = sem("l_turned")
    l_copied = sem("l_copied")
    l_mm = sem("l_mm")
    h_made = sem("h_made")
    stats_made = sem("stats_made")
    mean_made = sem("mean_made")
    half_made = sem("half_made")
    var_made = sem("var_made")
    rstd_made = sem("rstd_made")
    xn_made = sem("xn_made")
    x_turned = sem("x_turned")
    x_hi = sem("x_hi")
    x_lo = sem("x_lo")
    h_stored = [sem(f"h_stored{u}") for u in range(2)]
    w_stored = sem("w_stored")

    block = ctx.enter_context(nc.Block())

    @block.sync
    def _(sp):
        sp.dma_start(tok_ids[:, :].rearrange("p (b t) -> p b t", b=B), x.rearrange("b (t p) -> p b t", p=P), allow_slow_non_contiguous=True).then_inc(ids_in, 16)
        sp.dma_start(lb[:, :], lora_b[:, :]).then_inc(lb_in, 16)
        for k in range(4):
            src = w_qkv[k * D:(k + 1) * D, :] if k < 3 else w_out[:, :]
            sp.dma_start(wrows[:, k, :, :], src.rearrange("(g p) n -> p g n", p=P)).then_inc(w_in[k], 16)
        for k in range(3):
            sp.wait_ge(w_lo, G * (k + 1))
            sp.dma_start(wqkvT_dram[k].rearrange("g p n -> p g n"),
                         wT[:, k, :, :, :].bitcast(F32).rearrange("p g a n -> p g (a n)")
                         ).then_inc(w_stored, 16)
        sp.wait_ge(w_lo, 4 * G)
        sp.dma_start(woT_dram[:, :], woT[:, :, :, :].bitcast(F32).rearrange("p a k n -> p (a k n)")
                     ).then_inc(w_stored, 16)

        def store_h(n, u):
            sp.wait_ge(h_made, n + 1)
            sp.dma_start(h_dram[ds(n, 1), :, :].rearrange("a p n -> p (a n)"), hid[:, u, :]
                         ).then_inc(h_stored[u], 16)

        with sp.Fori(0, NT // 2) as t:
            for u in range(2):
                store_h(t * 2 + u, u)
        sp.wait_ge(w_stored, 64)
        for u in range(2):
            sp.wait_ge(h_stored[u], 16 * NT // 2)

    @block.gpsimd
    def _(pool):
        def gather(n, u):
            if n >= 2:
                pool.wait_ge(h_made, n - 1)
                pool.wait_ge(l_turned, n - 1)
            for rows, table in ((emb, tok_w), (lrow, lora_a)):
                pool.indirect_dma_start(
                    out=rows[:, u, :], out_offset=None, in_=table,
                    in_offset=bass.IndirectOffsetOnAxis(ap=tok_ids[:, n:n + 1], axis=0),
                ).then_inc(emb_in[u], 16)

        def make_rstd(n, u):
            pool.wait_ge(mean_made, n + 1)
            pool.tensor_tensor(var_eps[:, u:u + 1], mean_var[:, u, 1:2], eps[:, :], ALU.add
                               ).then_inc(var_made, 1)
            pool.wait_ge(var_made, n + 1)
            pool.tensor_tensor(rstd[:, u:u + 1], var_eps[:, u:u + 1], minus_half[:, :], ALU.pow
                               ).then_inc(rstd_made, 1)

        pool.memset(minus_half[:, :], -0.5).then_inc(half_made, 1)
        pool.memset(eps[:, :], EPS).then_inc(half_made, 1)
        pool.wait_ge(half_made, 2)
        pool.wait_ge(ids_in, 16)
        gather(0, 0)
        for n in range(NT):
            if n + 1 < NT:
                gather(n + 1, (n + 1) % 2)
            make_rstd(n, n % 2)

    def in_flight(n, u):
        return (n - u) * 16 + 32

    @block.tensor
    def _(pe):
        for k in range(4):
            pe.wait_ge(w_in[k], 16)
            for g in range(G):
                n = k * G + g
                if n >= 2:
                    pe.wait_ge(w_lo, n - 1)
                for c in range(KC):
                    mm = pe.transpose(wturned[n % 2][:, c * P:(c + 1) * P],
                                      wrows[:, k, g, c * P:(c + 1) * P], identf[:, :])
                mm.then_inc(w_turned, 1)

        def lora_tile(n, u):
            pe.wait_ge(emb_in[u], in_flight(n, u))
            if later(n, 1):
                pe.wait_ge(l_copied, n)
            pe.transpose(lturned[0:RANK, 0:P], lrow[:, u, :], identf[:, :]).then_inc(l_turned, 1)
            pe.wait_ge(l_copied, n + 1)
            if later(n, 1):
                pe.wait_ge(h_made, n)
            pe.matmul(lora[:, :], lrowT[:, u, :], lb[:, :], start=True, stop=True).then_inc(l_mm, 1)

        def turn_tile(n, u):
            pe.wait_ge(xn_made, n + 1)
            if later(n, 2):
                pe.wait_ge(x_lo, n - 1)
            for c in range(KC):
                mm = pe.transpose(turned[u][:, c * P:(c + 1) * P], xn[:, u, c * P:(c + 1) * P],
                                  identf[:, :])
            mm.then_inc(x_turned, 1)

        pe.wait_ge(lb_in, 16)
        lora_tile(0, 0)
        lora_tile(1, 1)
        turn_tile(0, 0)
        with pe.Fori(1, NT // 2) as t:
            lora_tile(t * 2, 0)
            turn_tile(t * 2 - 1, 1)
            lora_tile(t * 2 + 1, 1)
            turn_tile(t * 2, 0)
        turn_tile(NT - 1, 1)

    def w_parts(n):
        k, g = n // G, n % G
        if k < 3:
            return wT[:, k, g, 0, :], wT[:, k, g, 1, :]
        return woT[:, 0, :, g * P:(g + 1) * P], woT[:, 1, :, g * P:(g + 1) * P]

    def w_source(n):
        t = wturned[n % 2]
        return t[:, :] if n // G < 3 else t[:, :].rearrange("p (k c) -> p k c", c=P)

    def x_part(part, n):
        return xT[:, part, :, ds(n * P, P)]

    @block.scalar
    def _(act):
        for n in range(4 * G):
            act.wait_ge(w_turned, n + 1)
            act.activation(w_parts(n)[0], w_source(n), ACT.Copy).then_inc(w_hi, 1)

        def copy_l(n, u):
            act.wait_ge(l_turned, n + 1)
            if later(n, 2):
                act.wait_ge(l_mm, n - 1)
            act.activation(lrowT[:, u, :], lturned[0:RANK, 0:P], ACT.Copy).then_inc(l_copied, 1)

        def high(n, u):
            act.wait_ge(x_turned, n + 1)
            act.activation(x_part(0, n), turned[u][:, :].rearrange("p (k c) -> p k c", c=P),
                           ACT.Copy).then_inc(x_hi, 1)

        copy_l(0, 0)
        copy_l(1, 1)
        high(0, 0)
        with act.Fori(1, NT // 2) as t:
            copy_l(t * 2, 0)
            high(t * 2 - 1, 1)
            copy_l(t * 2 + 1, 1)
            high(t * 2, 0)
        high(NT - 1, 1)

    @block.vector
    def _(dve):
        for n in range(4 * G):
            dve.wait_ge(w_hi, n + 1)
            dve.tensor_tensor(w_parts(n)[1], w_source(n), w_parts(n)[0].bitcast(F32), ALU.subtract
                              ).then_inc(w_lo, 1)

        def hidden(n, u):
            dve.wait_ge(l_mm, n + 1)
            dve.wait_ge(emb_in[u], in_flight(n, u))
            if later(n, 2):
                dve.wait_ge(h_stored[u], (n - u) * 8)
            dve.scalar_tensor_tensor(out=hid[:, u, :], in0=lora[:, :], scalar=LORA_SCALING,
                                     in1=emb[:, u, :], op0=ALU.mult, op1=ALU.add).then_inc(h_made, 1)
            dve.wait_ge(h_made, n + 1)
            dve.bn_stats(stats[:, u, :], hid[:, u, :]).then_inc(stats_made, 1)
            dve.wait_ge(stats_made, n + 1)

        def aggregate(n, u):
            dve.bn_aggr(mean_var[:, u, :], stats[:, u, :]).then_inc(mean_made, 1)

        def normal(n, u):
            dve.wait_ge(rstd_made, n + 1)
            if later(n, 2):
                dve.wait_ge(x_turned, n - 1)
            dve.tensor_scalar(xn[:, u, :], hid[:, u, :], mean_var[:, u, 0:1], rstd[:, u:u + 1],
                              ALU.subtract, ALU.mult).then_inc(xn_made, 1)

        def low(n, u):
            dve.wait_ge(x_hi, n + 1)
            dve.tensor_tensor(x_part(1, n), turned[u][:, :].rearrange("p (k c) -> p k c", c=P),
                              x_part(0, n).bitcast(F32), ALU.subtract).then_inc(x_lo, 1)

        hidden(0, 0)
        aggregate(0, 0)
        hidden(1, 1)
        normal(0, 0)
        aggregate(1, 1)
        with dve.Fori(1, NT // 2) as t:
            hidden(t * 2, 0)
            normal(t * 2 - 1, 1)
            aggregate(t * 2, 0)
            low(t * 2 - 2, 0)
            hidden(t * 2 + 1, 1)
            normal(t * 2, 0)
            aggregate(t * 2 + 1, 1)
            low(t * 2 - 1, 1)
        normal(NT - 1, 1)
        low(NT - 2, 0)
        low(NT - 1, 1)


def attend(nc, ctx, identf, identb, onesf, xT, wqkvT_dram, attnT_dram):
    sb, ps, sem = allocators(nc, ctx, "attn")
    w = sb("w", [P, 3, 2, KC, P], F32R)
    qk = sb("qk", [P, 2, 2, S], F32R)
    vT = sb("vT", [P, S])
    q_stack = [sb(f"q_stack{u}", [P, GH, S], F32R) for u in range(2)]
    k_stack = [sb(f"k_stack{u}", [P, GH, S], F32R) for u in range(2)]
    v = [sb(f"v{u}", [P, QT, P]) for u in range(2)]
    probs = sb("probs", [P, 2, GH, C])
    part_max = sb("part_max", [P, 2, GH, QT])
    neg_max = sb("neg_max", [P, GH, QT])
    neg_max_parts = sb("neg_max_parts", [P, 2, GH, QT])
    max_rows = sb("max_rows", [2 * GH * QT, P])
    out_copy = sb("out_copy", [P, C])
    denom_copy = sb("denom_copy", [P, C])
    rdenom = sb("rdenom", [P, C])
    attnT = sb("attnT", [P, 2, C])
    go = sb("go", [P, 1])
    mask_keys = sb("mask_keys", [P, P], BF16)
    mask_queries = sb("mask_queries", [P, P], BF16)

    scoresT = [ps(f"scoresT{u}", [P, 2, C]) for u in range(2)]
    outT = ps("outT", [P, C])
    denom = ps("denom", [P, C])
    work = [ps(f"work{u}", [P, C]) for u in range(2)]

    masks_made = sem("masks_made")
    w_in = sem("w_in")
    work_made = sem("work_made")
    work_free = [sem(f"work_free{u}") for u in range(2)]
    qk_hi = sem("qk_hi")
    stack_in = [[sem(f"{y}_stack_in{u}") for y in ("q", "k", "k_pool")] for u in range(2)]
    go_made = sem("go_made")
    part_max_made = sem("part_max_made")
    neg_max_made = sem("neg_max_made")
    max_rows_in = [sem(f"max_rows_in{u}") for u in range(2)]
    scoresT_made = sem("scoresT_made")
    probs_made = sem("probs_made")
    probs_used = sem("probs_used")
    out_copied = sem("out_copied")
    rdenom_made = sem("rdenom_made")
    attn_made = sem("attn_made")
    attn_stored = [sem(f"attn_stored{u}") for u in range(2)]

    STACKED = [("q", (0, 1, 2)), ("k", (0,)), ("k", (1, 2))]
    RQ = 4
    QKV_SLOTS = [1, 3, 7, 10, 12, 14]
    STEPS = [(c, j, max(c * C, j * P), (c + 1) * C - max(c * C, j * P))
             for c in range(NC) for j in range((c + 1) * C // P)]
    NS = len(STEPS)
    SCORES = [(h, t, k0, min(C, (t + 1) * P - k0)) for h in range(GH) for t in range(QT)
              for k0 in range(0, (t + 1) * P, C)]
    PIECES = ([("q", c) for c in range(NC)] + [("k", c) for c in range(NC)]
              + [("v", c) for c in range(NC)] + [("vt", c) for c in range(NC)]
              + [("s", n) for n in range(len(SCORES))] + [("m", a) for a in range(2)])
    NP = len(PIECES)
    assert NP % 2 == 0
    NUMBER = {piece: n for n, piece in enumerate(PIECES)}
    NSC = len(SCORES)
    SLOTS = 4
    FIRST = PIECES[:NC]
    AT = [[] for _ in range(NS * SLOTS)]
    for slot, piece in zip(QKV_SLOTS, PIECES[NC:4 * NC]):
        AT[slot].append(piece)
    begin, end = QKV_SLOTS[-1] + 1, NS * SLOTS - 2
    for n in range(NSC):
        AT[begin + n * (end - begin) // NSC].append(("s", n))
    AT[-1] += PIECES[-2:]
    assert FIRST + [p for a in AT for p in a] == PIECES

    def ends_chunk(s, slot):
        if s == NS:
            return NC - 1
        if slot == 0 and s >= 2 and STEPS[s - 1][0] == STEPS[s - 2][0] + 1:
            return STEPS[s - 2][0]
        return None

    block = ctx.enter_context(nc.Block())

    def stacked(i, b, k):
        return (i - b) * (8 * GH * len(STACKED[k][1])) + 16 * GH * len(STACKED[k][1])

    def turns(eng, prepare, attend_slot):
        def half(ia, ip):
            if ip is not None:
                for piece in FIRST:
                    prepare(*ip, piece, NUMBER[piece])
            for slot in range(NS * SLOTS):
                if ia is not None:
                    attend_slot(*ia, slot // SLOTS, slot % SLOTS)
                if ip is not None:
                    for piece in AT[slot]:
                        prepare(*ip, piece, NUMBER[piece])
            if ia is not None:
                attend_slot(*ia, NS, 0)
        half(None, (0, 0, 0))
        half((0, 0, 0), (1, 1, 0))
        half((1, 1, 0), (2, 0, 1))
        with eng.Fori(1, G - 1) as g:
            half((g * 2, 0, g), (g * 2 + 1, 1, g))
            half((g * 2 + 1, 1, g), (g * 2 + 2, 0, g + 1))
        half((2 * G - 2, 0, G - 1), (2 * G - 1, 1, G - 1))
        half((2 * G - 1, 1, G - 1), None)

    def in_bank(i, n):
        return i * (NP // 2) + n // 2

    def stack_waits(eng, i, n):
        eng.wait_ge(work_free[1 - n % 2], in_bank(i, n - 1) + 1)
        if later(i, 2):
            eng.wait_ge(scoresT_made, (i - 1) * 2 * NS)
        eng.wait_ge(work_free[n % 2], in_bank(i, n) + 1)

    def stack(eng, b, which):
        kind, blocks = STACKED[which]
        y = "qk".index(kind)
        to = (q_stack, k_stack)[y][b]
        parts = ((0, 0, 1), (0, 1, 0))[y]
        for r in blocks:
            for h in range(GH):
                eng.dma_start(to[r * HD:(r + 1) * HD, h, :].bitcast(F32),
                              qk[h * HD:(h + 1) * HD, y, parts[r], :].bitcast(F32)
                              ).then_inc(stack_in[b][which], 16)

    @block.sync
    def _(sp):
        def load_w(g):
            if later(g, 1):
                sp.wait_ge(work_made, (g * 2 - 1) * NP + NUMBER["v", NC - 1] + 1)
            sp.dma_start(w[:, :, :, :, :].bitcast(F32).rearrange("p y a k c -> p y (a k c)"),
                         wqkvT_dram[:, ds(g, 1), :, :].rearrange("y g p n -> p (y g) n")
                         ).then_inc(w_in, 16)

        def prepare(i, b, g, piece, n):
            kind, c = piece
            u = n % 2
            if kind in "qk" and c == NC - 1:
                stack_waits(sp, i, n)
                stack(sp, b, "qk".index(kind))
            if kind == "v" and c == NC - 1 and b == 1:
                if not isinstance(g, int) or g < G - 1:
                    load_w(g + 1)
            if kind == "m" and c == 1:
                sp.wait_ge(work_free[1 - u], in_bank(i, n - 1) + 1)
                sp.wait_ge(work_free[u], in_bank(i, n) + 1)
                for part in range(2):
                    sp.dma_start(q_stack[b][3 * HD + part:3 * HD + part + 1, :, :].bitcast(F32)
                                 .rearrange("a h (t q) -> a (h t) q", q=P),
                                 max_rows[part * GH * QT:(part + 1) * GH * QT, :]
                                 ).then_inc(max_rows_in[b], 16)

        def attend_slot(i, b, g, s, slot):
            c = ends_chunk(s, slot)
            if c is not None:
                sp.wait_ge(attn_made, i * NC + c + 1)
                sp.dma_start(attnT_dram[ds(g, 1), :, b * S + c * C:b * S + (c + 1) * C]
                             .rearrange("a p n -> p (a n)"), attnT[:, c, :]
                             ).then_inc(attn_stored[c], 16)

        load_w(0)
        turns(sp, prepare, attend_slot)
        for c in range(NC):
            sp.wait_ge(attn_stored[c], 16 * 2 * G)

    @block.gpsimd
    def _(pool):
        for n, (out, value) in enumerate(
                [(mask_keys[:, :], 0.0), (mask_queries[:, :], 0.0), (part_max[:, 1, :, :], 3.0e38)]
                + [(k_stack[u][3 * HD:3 * HD + 2, :, :].bitcast(F32), 1.0) for u in range(2)]):
            pool.memset(out, value).then_inc(masks_made, 1)
            pool.wait_ge(masks_made, n + 1)
        pool.affine_select(out=mask_keys[:, :], in_=mask_keys[:, :], compare_op=ALU.is_ge,
                           fill=MASKED, base=0, pattern=[[-1, P]], channel_multiplier=1
                           ).then_inc(masks_made, 1)
        pool.wait_ge(masks_made, 6)
        pool.affine_select(out=mask_queries[:, :], in_=mask_queries[:, :], compare_op=ALU.is_ge,
                           fill=MASKED, base=0, pattern=[[1, P]], channel_multiplier=-1
                           ).then_inc(masks_made, 1)

        def prepare(i, b, g, piece, n):
            kind, c = piece
            if kind == "k" and c == NC - 1:
                if later(i, 1):
                    pool.wait_ge(go_made, i)
                stack_waits(pool, i, n)
                pool.tensor_tensor(go[:, :], onesf[:, 0:1], onesf[:, 0:1], ALU.mult
                                   ).then_inc(go_made, 1)
                stack(pool, b, 2)

        def attend_slot(i, b, g, s, slot):
            c = ends_chunk(s, slot)
            if c is not None:
                pool.wait_ge(rdenom_made, i * NC * RQ + (c + 1) * RQ)
                pool.wait_ge(out_copied, (i * NC + c) * 2 + 2)
                if later(i, 1):
                    pool.wait_ge(attn_stored[c], i * 16)
                pool.tensor_tensor(attnT[:, c, :], out_copy[:, :], rdenom[:, :], ALU.mult
                                   ).then_inc(attn_made, 1)

        turns(pool, prepare, attend_slot)

    @block.tensor
    def _(pe):
        def prepare(i, b, g, piece, n):
            kind, c = piece
            u = n % 2
            bank = work[u]
            if later(i, 1) or n >= 2:
                pe.wait_ge(work_free[u], in_bank(i, n))
            if kind in "qkv":
                y = "qkv".index(kind)
                if n == 0:
                    pe.wait_ge(w_in, g * 16 + 16)
                terms = [(0, 0), (0, 1), (1, 0)]
                for m, (wp, xp) in enumerate(terms):
                    for kc in range(KC):
                        mm = pe.matmul(bank[:, :], w[:, y, wp, kc, :],
                                       xT[:, xp, kc, b * S + c * C:b * S + (c + 1) * C],
                                       start=(m == 0 and kc == 0), stop=(m == 2 and kc == KC - 1))
            elif kind == "vt":
                if c == 0:
                    pe.wait_ge(work_free[1 - u], in_bank(i, n - 1) + 1)
                for t in range(4):
                    mm = pe.transpose(bank[:, t * P:(t + 1) * P], vT[:, (4 * c + t) * P:(4 * c + t + 1) * P],
                                      identf[:, :])
            elif kind == "s":
                h, t, k0, nk = SCORES[c]
                if c == 0:
                    for k in range(3):
                        pe.wait_ge(stack_in[b][k], stacked(i, b, k))
                diagonal = k0 + nk == (t + 1) * P
                mm = pe.matmul(bank[:, 0:nk], q_stack[b][0:3 * HD, h, t * P:(t + 1) * P],
                               k_stack[b][0:3 * HD, h, k0:k0 + nk], start=True, stop=not diagonal)
                if diagonal:
                    mm = pe.matmul(bank[:, nk - P:nk], identb[:, :], mask_keys[:, :],
                                   start=False, stop=True)
            else:
                pe.wait_ge(neg_max_made, i * 3 + 3)
                mm = pe.transpose(bank[0:GH * QT, 0:P], neg_max_parts[:, c, :, :].rearrange("p h t -> p (h t)"),
                                  identf[:, :])
            mm.then_inc(work_made, 1)

        def values(i, b, s, ones):
            c, j, q0, nq = STEPS[s]
            if not ones:
                if j == 0 and (later(i, 1) or c > 0):
                    pe.wait_ge(out_copied, (i * NC + c) * 2)
                if s == 0:
                    for n in range(2):
                        m = NUMBER["vt", n]
                        pe.wait_ge(work_free[m % 2], in_bank(i, m) + 1)
                pe.wait_ge(probs_made, i * 2 * NS + 2 * s + 2)
            for h in range(GH):
                mm = pe.matmul((denom if ones else outT)[h * HD:(h + 1) * HD, q0 - c * C:q0 - c * C + nq],
                               onesf[:, 0:HD] if ones else v[b][:, j, h * HD:(h + 1) * HD],
                               probs[:, s % 2, h, 0:nq], start=(j == 0),
                               stop=(j == (c + 1) * C // P - 1))
            if ones:
                mm.then_inc(probs_used, 1)

        def attend_slot(i, b, g, s, slot):
            if s == NS:
                values(i, b, NS - 1, False)
                values(i, b, NS - 1, True)
                return
            c, j, q0, nq = STEPS[s]
            if slot >= 2:
                if s >= 1:
                    values(i, b, s - 1, slot == 3)
                return
            hp = slot
            if s == 0 and hp == 0:
                pe.wait_ge(max_rows_in[b], (i - b) * 16 + 32)
            if later(i, 1) or s >= 1:
                pe.wait_ge(probs_made, i * 2 * NS + max(2 * s + hp - 1, 0))
            for h2 in range(2):
                h = hp * 2 + h2
                diagonal = j * P >= c * C
                mm = pe.matmul(scoresT[hp][:, h2, 0:nq], k_stack[b][0:3 * HD + 2, h, j * P:(j + 1) * P],
                               q_stack[b][0:3 * HD + 2, h, q0:q0 + nq], start=True, stop=not diagonal)
                if diagonal:
                    mm = pe.matmul(scoresT[hp][:, h2, 0:P], identb[:, :], mask_queries[:, :],
                                   start=False, stop=True)
            mm.then_inc(scoresT_made, 1)

        pe.wait_ge(masks_made, 7)
        turns(pe, prepare, attend_slot)

    @block.scalar
    def _(act):
        def prepare(i, b, g, piece, n):
            kind, c = piece
            u = n % 2
            if kind in "qk":
                y = "qk".index(kind)
                act.wait_ge(work_made, i * NP + n + 1)
                if c == 0 and later(i, 1):
                    for k in ((0,), (1, 2))[y]:
                        act.wait_ge(stack_in[1 - b][k], stacked(i - 1, 1 - b, k))
                act.activation(qk[:, y, 0, c * C:(c + 1) * C], work[u][:, :], ACT.Copy).then_inc(qk_hi, 1)
            elif kind == "v":
                act.wait_ge(work_made, i * NP + n + 1)
                act.activation(vT[:, c * C:(c + 1) * C], work[u][:, :], ACT.Copy
                               ).then_inc(work_free[u], 1)
            elif kind == "vt":
                act.wait_ge(work_made, i * NP + n + 1)
                act.activation(v[b][:, 4 * c:4 * c + 4, :],
                               work[u][:, :].rearrange("p (t d) -> p t d", d=P), ACT.Copy
                               ).then_inc(work_free[u], 1)

        def attend_slot(i, b, g, s, slot):
            if s < NS and slot < 2:
                c, j, q0, nq = STEPS[s]
                hp = slot
                act.wait_ge(scoresT_made, i * 2 * NS + 2 * s + hp + 1)
                if later(i, 1) or s >= 2:
                    act.wait_ge(probs_used, i * NS + max(s - 1, 0))
                act.activation(probs[:, s % 2, hp * 2:hp * 2 + 2, 0:nq], scoresT[hp][:, :, 0:nq],
                               ACT.Exp, scale=SM_SCALE).then_inc(probs_made, 1)
            c = ends_chunk(s, slot)
            if c is not None:
                end = NS if s == NS else s - 1
                act.wait_ge(probs_used, i * NS + end)
                if later(i, 1) or c > 0:
                    act.wait_ge(rdenom_made, (i * NC + c) * RQ)
                act.activation(denom_copy[:, :], denom[:, :], ACT.Copy).then_inc(out_copied, 1)
                if later(i, 1) or c > 0:
                    act.wait_ge(attn_made, i * NC + c)
                act.activation(out_copy[:, :], outT[:, :], ACT.Copy).then_inc(out_copied, 1)

        turns(act, prepare, attend_slot)

    @block.vector
    def _(dve):
        def prepare(i, b, g, piece, n):
            kind, c = piece
            u = n % 2
            if kind in "qk":
                y = "qk".index(kind)
                dve.wait_ge(qk_hi, i * 4 + y * 2 + c + 1)
                dve.tensor_tensor(qk[:, y, 1, c * C:(c + 1) * C], work[u][:, :],
                                  qk[:, y, 0, c * C:(c + 1) * C].bitcast(F32), ALU.subtract
                                  ).then_inc(work_free[u], 1)
            elif kind == "s":
                h, t, k0, nk = SCORES[c]
                if c == 0:
                    dve.wait_ge(masks_made, 7)
                    if later(i, 1):
                        dve.wait_ge(neg_max_made, i * 3)
                dve.wait_ge(work_made, i * NP + n + 1)
                dve.tensor_reduce(part_max[:, k0 // C, h, t:t + 1], work[u][:, 0:nk], AX_X, ALU.max,
                                  negate=True).then_inc(work_free[u], 1)
                if c == NSC - 1:
                    dve.wait_ge(work_free[u], in_bank(i, n) + 1)
                    dve.wait_ge(work_free[1 - u], in_bank(i, n - 1) + 1)
                    if later(i, 1):
                        dve.wait_ge(work_made, i * NP)
                    dve.tensor_tensor(neg_max[:, :, :], part_max[:, 0, :, :], part_max[:, 1, :, :],
                                      ALU.min).then_inc(neg_max_made, 1)
                    dve.wait_ge(neg_max_made, i * 3 + 1)
                    dve.tensor_copy(neg_max_parts[:, 0, :, :].bitcast(F32R), neg_max[:, :, :]
                                    ).then_inc(neg_max_made, 1)
                    dve.wait_ge(neg_max_made, i * 3 + 2)
                    dve.tensor_tensor(neg_max_parts[:, 1, :, :], neg_max[:, :, :],
                                      neg_max_parts[:, 0, :, :], ALU.subtract).then_inc(neg_max_made, 1)
            elif kind == "m":
                dve.wait_ge(work_made, i * NP + n + 1)
                if c == 0 and later(i, 1):
                    dve.wait_ge(max_rows_in[1 - b], (i - 1 - (1 - b)) * 16 + 32)
                dve.tensor_copy(max_rows[c * GH * QT:(c + 1) * GH * QT, :], work[u][0:GH * QT, 0:P]
                                ).then_inc(work_free[u], 1)

        def attend_slot(i, b, g, s, slot):
            def reciprocals(c, k):
                if k == 0:
                    dve.wait_ge(out_copied, (i * NC + c) * 2 + 1)
                    if later(i, 1) or c > 0:
                        dve.wait_ge(attn_made, i * NC + c)
                cols = slice(k * C // RQ, (k + 1) * C // RQ)
                dve.reciprocal(rdenom[:, cols], denom_copy[:, cols]).then_inc(rdenom_made, 1)

            if s == NS:
                for k in range(RQ):
                    reciprocals(NC - 1, k)
            elif slot in (1, 3):
                for c in range(NC - 1):
                    after = next(m for m in range(NS) if ends_chunk(m, 0) == c)
                    k = (s - after) * 2 + slot // 2
                    if 0 <= k < RQ:
                        reciprocals(c, k)

        turns(dve, prepare, attend_slot)


def feed(nc, ctx, identb, h_dram, attnT_dram, wguT_dram, wdT_dram, srow_dram, woT_dram, out):
    sb, ps, sem = allocators(nc, ctx, "feed")
    woT = sb("woT", [P, 2, KC, D], F32R)
    wguT = sb("wguT", [P, KC, 2 * I_FF], BF16)
    wdT = sb("wdT", [P, NI, D], BF16)
    srow = sb("srow", [P, 2 * I_FF + D])
    attn_in = sb("attn_in", [P, 2, KC, P])
    h_in = sb("h_in", [P, 2, D])
    attn = [[sb(f"attn{u}{part}", [P, KC, P], F32R) for part in range(2)] for u in range(2)]
    h2 = sb("h2", [P, 2, D])
    h2_kept = sb("h2_kept", [P, 2, D])
    stats = sb("stats", [P, 2, 6])
    mean_var = sb("mean_var", [P, 2, 2])
    var_eps = sb("var_eps", [P, 2])
    rstd = sb("rstd", [P, 2])
    minus_half = sb("minus_half", [P, 1])
    eps = sb("eps", [P, 1])
    xn = sb("xn", [P, 2, D])
    x_max = sb("x_max", [P, 2])
    x_scale = sb("x_scale", [P, 2])
    x_rscale = sb("x_rscale", [P, 2])
    x_scaled = sb("x_scaled", [P, 2, D])
    x_magic = sb("x_magic", [P, 2, D], U32)
    x_rounded = sb("x_rounded", [P, 2, D], BF16)
    xT = [sb(f"xT{u}", [P, KC, P], BF16) for u in range(2)]
    gate = sb("gate", [P, I_FF])
    up = sb("up", [P, I_FF])
    t_max = sb("t_max", [P, 2])
    t_scale = sb("t_scale", [P, 2])
    t_rscale = sb("t_rscale", [P, 2])
    t_scaled = sb("t_scaled", [P, I_FF])
    t_magic = sb("t_magic", [P, I_FF], U32)
    t_rounded = sb("t_rounded", [P, I_FF], BF16)
    tT = sb("tT", [P, NI, P], BF16)
    y_down = sb("y_down", [P, D])
    y = sb("y", [P, 2, D])

    proj = ps("proj", [P, D])
    down = ps("down", [P, D])
    gu = [ps(f"gu{k}", [P, D]) for k in range(4)]
    t_turned = ps("t_turned", [P, 2048], BF16)
    x_turned = down[:, 0:D // 2].bitcast(BF16)

    woT_in = sem("woT_in")
    wguT_in = sem("wguT_in")
    wdT_in = sem("wdT_in")
    srow_in = sem("srow_in")
    consts_made = sem("consts_made")
    attn_in_ = [sem(f"attn_in{u}") for u in range(2)]
    h_in_ = [sem(f"h_in{u}") for u in range(2)]
    attn_hi = sem("attn_hi")
    attn_lo = sem("attn_lo")
    proj_made = sem("proj_made")
    h2_made = sem("h2_made")
    h2_kept_made = sem("h2_kept_made")
    stats_made = sem("stats_made")
    mean_made = sem("mean_made")
    var_made = sem("var_made")
    rstd_made = sem("rstd_made")
    xn_made = sem("xn_made")
    x_max_made = sem("x_max_made")
    x_scale_made = sem("x_scale_made")
    x_rscale_made = sem("x_rscale_made")
    x_scaled_made = sem("x_scaled_made")
    x_power_made = sem("x_power_made")
    x_magic_made = sem("x_magic_made")
    x_sum_made = sem("x_sum_made")
    x_rounded_made = sem("x_rounded_made")
    x_turned_made = sem("x_turned_made")
    xT_made = sem("xT_made")
    gu_made = sem("gu_made")
    gu_used = sem("gu_used")
    silu_made = sem("silu_made")
    t_made = sem("t_made")
    t_max_made = sem("t_max_made")
    t_scale_made = sem("t_scale_made")
    t_rscale_made = sem("t_rscale_made")
    t_scaled_made = sem("t_scaled_made")
    t_power_made = sem("t_power_made")
    t_magic_made = sem("t_magic_made")
    t_sum_made = sem("t_sum_made")
    t_rounded_made = sem("t_rounded_made")
    t_turned_made = sem("t_turned_made")
    tT_made = sem("tT_made")
    down_made = sem("down_made")
    y_down_made = sem("y_down_made")
    y_made = sem("y_made")
    y_stored = [sem(f"y_stored{u}") for u in range(2)]

    out_rows = out.rearrange("b s d -> (b s) d")
    block = ctx.enter_context(nc.Block())

    def turns(eng, turn):
        turn(-2, 0, True, False, False)
        turn(-1, 1, True, True, False)
        for n in range(2):
            turn(n, n, True, True, True)
        with eng.Fori(1, NT // 2 - 2) as t:
            for u in range(2):
                turn(t * 2 + u, u, True, True, True)
        for n in range(NT - 4, NT - 2):
            turn(n, n % 2, True, True, True)
        turn(NT - 2, 0, False, True, True)
        turn(NT - 1, 1, False, False, True)

    def loaded(n, u):
        return (n - u) * 8 + 16

    @block.sync
    def _(sp):
        def load(n, u):
            if later(n, 2):
                sp.wait_ge(attn_lo, n - 1)
            sp.dma_start(attn_in[:, u, :, :],
                         attnT_dram[:, :, ds(n * P, P)].rearrange("g p n -> p g n")
                         ).then_inc(attn_in_[u], 16)
            if later(n, 2):
                sp.wait_ge(h2_made, n - 1)
            sp.dma_start(h_in[:, u, :], h_dram[ds(n, 1), :, :].rearrange("a p n -> p (a n)")
                         ).then_inc(h_in_[u], 16)

        def store(n, u):
            sp.wait_ge(y_made, n + 1)
            sp.dma_start(out_rows[ds(n * P, P), :], y[:, u, :]).then_inc(y_stored[u], 16)

        load(0, 0)
        sp.dma_start(woT[:, :, :, :].bitcast(F32).rearrange("p a k n -> p (a k n)"), woT_dram[:, :]
                     ).then_inc(woT_in, 16)
        load(1, 1)
        sp.dma_start(wguT[:, :, :].rearrange("p k n -> p (k n)"), wguT_dram[:, :]).then_inc(wguT_in, 16)
        sp.dma_start(srow[:, :], srow_dram[:, :]).then_inc(srow_in, 16)
        sp.dma_start(wdT[:, :, :].rearrange("p k n -> p (k n)"), wdT_dram[:, :]).then_inc(wdT_in, 16)
        load(2, 0)
        for n in range(2):
            load(n + 3, 1 - n)
            store(n, n)
        with sp.Fori(1, NT // 2 - 2) as t:
            for u in range(2):
                load(t * 2 + u + 3, 1 - u)
                store(t * 2 + u, u)
        for n in range(NT - 4, NT):
            if n + 3 < NT:
                load(n + 3, 1 - n % 2)
            store(n, n % 2)
        for u in range(2):
            sp.wait_ge(y_stored[u], 16 * NT // 2)

    @block.gpsimd
    def _(pool):
        def low(n, u):
            pool.wait_ge(attn_hi, n + 1)
            if later(n, 2):
                pool.wait_ge(proj_made, n - 1)
            pool.tensor_tensor(attn[u][1][:, :, :], attn_in[:, u, :, :],
                               attn[u][0][:, :, :].bitcast(F32), ALU.subtract).then_inc(attn_lo, 1)

        def turn(n, u, a, b, c):
            if a:
                m = n + 2
                pool.wait_ge(mean_made, m + 1)
                pool.tensor_tensor(var_eps[:, u:u + 1], mean_var[:, u, 1:2], eps[:, :], ALU.add
                                   ).then_inc(var_made, 1)
                pool.wait_ge(var_made, m + 1)
                pool.tensor_tensor(rstd[:, u:u + 1], var_eps[:, u:u + 1], minus_half[:, :], ALU.pow
                                   ).then_inc(rstd_made, 1)
                pool.wait_ge(x_magic_made, m + 1)
                pool.tensor_tensor(x_scaled[:, u, :], x_scaled[:, u, :],
                                   x_magic[:, u, :].bitcast(F32), ALU.add).then_inc(x_sum_made, 1)
                pool.wait_ge(x_sum_made, m + 1)
                if later(m, 2):
                    pool.wait_ge(x_turned_made, m - 1)
                pool.tensor_tensor(x_rounded[:, u, :], x_scaled[:, u, :],
                                   x_magic[:, u, :].bitcast(F32), ALU.subtract
                                   ).then_inc(x_rounded_made, 1)
                if not isinstance(n, int) or m + 1 < NT:
                    low(m + 1, 1 - u)
            if b:
                m = n + 1
                pool.wait_ge(t_magic_made, m + 1)
                pool.tensor_tensor(t_scaled[:, :], t_scaled[:, :], t_magic[:, :].bitcast(F32), ALU.add
                                   ).then_inc(t_sum_made, 1)
                pool.wait_ge(t_sum_made, m + 1)
                if later(m, 1):
                    pool.wait_ge(t_turned_made, m)
                pool.tensor_tensor(t_rounded[:, :], t_scaled[:, :], t_magic[:, :].bitcast(F32),
                                   ALU.subtract).then_inc(t_rounded_made, 1)
            if c:
                pool.wait_ge(y_down_made, n + 1)
                pool.wait_ge(h2_kept_made, n + 1)
                if later(n, 2):
                    pool.wait_ge(y_stored[u], (n - u) * 8)
                pool.tensor_tensor(y[:, u, :], y_down[:, :],
                                   h2_kept[:, u, :], ALU.add).then_inc(y_made, 1)

        pool.memset(minus_half[:, :], -0.5).then_inc(consts_made, 1)
        pool.memset(eps[:, :], EPS).then_inc(consts_made, 1)
        pool.wait_ge(consts_made, 2)
        low(0, 0)
        turns(pool, turn)

    @block.scalar
    def _(act):
        def high(n, u):
            act.wait_ge(attn_in_[u], loaded(n, u))
            if later(n, 2):
                act.wait_ge(proj_made, n - 1)
            act.activation(attn[u][0][:, :, :], attn_in[:, u, :, :], ACT.Copy).then_inc(attn_hi, 1)

        def turn(n, u, a, b, c):
            if b:
                m = n + 1
                act.wait_ge(x_turned_made, m + 1)
                if later(m, 2):
                    act.wait_ge(gu_made, (m - 1) * NGC)
                act.activation(xT[1 - u][:, :, :], x_turned.rearrange("p (k c) -> p k c", c=P),
                               ACT.Copy).then_inc(xT_made, 1)
                if later(m, 2):
                    act.wait_ge(y_made, m - 1)
                act.activation(h2_kept[:, 1 - u, :], h2[:, 1 - u, :], ACT.Copy
                               ).then_inc(h2_kept_made, 1)
                for half in range(2):
                    act.wait_ge(gu_used, m * NGC + 2 * half + 2)
                    act.activation(gate[:, half * 2 * GC:(half + 1) * 2 * GC],
                                   gate[:, half * 2 * GC:(half + 1) * 2 * GC], ACT.Silu
                                   ).then_inc(silu_made, 1)
            if a:
                m = n + 2
                act.wait_ge(x_rscale_made, m + 1)
                if later(m, 2):
                    act.wait_ge(x_rounded_made, m - 1)
                act.activation(x_scaled[:, u, :], xn[:, u, :], ACT.Copy, scale=x_rscale[:, u:u + 1]
                               ).then_inc(x_scaled_made, 1)
                if not isinstance(n, int) or m + 1 < NT:
                    high(m + 1, 1 - u)
            if c:
                act.wait_ge(t_turned_made, n + 1)
                if later(n, 1):
                    act.wait_ge(down_made, n)
                act.activation(tT[:, :, :], t_turned[:, 0:I_FF].rearrange("p (k c) -> p k c", c=P),
                               ACT.Copy).then_inc(tT_made, 1)
            if b:
                m = n + 1
                act.wait_ge(t_rscale_made, m + 1)
                if later(m, 1):
                    act.wait_ge(t_rounded_made, m)
                act.activation(t_scaled[:, :], up[:, :], ACT.Copy, scale=t_rscale[:, 1 - u:2 - u]
                               ).then_inc(t_scaled_made, 1)

        high(0, 0)
        turns(act, turn)

    @block.vector
    def _(dve):
        def turn(n, u, a, b, c):
            v = 1 - u

            def gate_up(k):
                m = n + 1
                dve.wait_ge(gu_made, m * NGC + k + 1)
                if k == 0 and later(m, 1):
                    dve.wait_ge(t_scaled_made, m)
                cols = slice(k * GC, (k + 1) * GC)
                dve.scalar_tensor_tensor(out=gate[:, cols], in0=gu[2 * (k % 2)][:, 0:GC],
                                         scalar=x_scale[:, v:v + 1], in1=srow[:, k * GC:(k + 1) * GC],
                                         op0=ALU.mult, op1=ALU.mult)
                dve.scalar_tensor_tensor(out=up[:, cols], in0=gu[2 * (k % 2) + 1][:, 0:GC],
                                         scalar=x_scale[:, v:v + 1],
                                         in1=srow[:, I_FF + k * GC:I_FF + (k + 1) * GC],
                                         op0=ALU.mult, op1=ALU.mult).then_inc(gu_used, 1)

            if a:
                m = n + 2
                dve.wait_ge(h_in_[u], loaded(m, u))
                dve.wait_ge(proj_made, m + 1)
                if later(m, 2):
                    dve.wait_ge(h2_kept_made, m - 1)
                row = h2[:, u, :]
                dve.tensor_tensor(row, proj[:, :], h_in[:, u, :], ALU.add).then_inc(h2_made, 1)
                dve.wait_ge(h2_made, m + 1)
                dve.bn_stats(stats[:, u, :], row).then_inc(stats_made, 1)
                dve.wait_ge(stats_made, m + 1)
            if b:
                gate_up(0)
            if a:
                if not b:
                    dve.tensor_copy(x_max[:, u:u + 1], stats[:, u, 0:1]).then_inc(x_max_made, 1)
                dve.bn_aggr(mean_var[:, u, :], stats[:, u, :]).then_inc(mean_made, 1)
            if b:
                gate_up(1)
            if a:
                m = n + 2
                dve.wait_ge(rstd_made, m + 1)
                if later(m, 2):
                    dve.wait_ge(x_scaled_made, m - 1)
                dve.tensor_scalar(xn[:, u, :], row, mean_var[:, u, 0:1], rstd[:, u:u + 1],
                                  ALU.subtract, ALU.mult).then_inc(xn_made, 1)
            if b:
                gate_up(2)
            if a:
                dve.wait_ge(xn_made, m + 1)
                dve.tensor_reduce(x_max[:, u:u + 1], xn[:, u, :], AX_X, ALU.max,
                                  apply_absolute_value=True).then_inc(x_max_made, 1)
                dve.wait_ge(x_max_made, m + 2)
                dve.tensor_scalar(x_scale[:, u:u + 1], x_max[:, u:u + 1], 1.0 / FP8_MAX, None,
                                  ALU.mult).then_inc(x_scale_made, 1)
                dve.wait_ge(x_scale_made, m + 1)
                dve.reciprocal(x_rscale[:, u:u + 1], x_scale[:, u:u + 1]).then_inc(x_rscale_made, 1)
            if b:
                gate_up(3)
            if a:
                dve.wait_ge(x_scaled_made, m + 1)
                if later(m, 2):
                    dve.wait_ge(x_rounded_made, m - 1)
                dve.tensor_scalar(x_magic[:, u, :], x_scaled[:, u, :].bitcast(U32), 0x7F800000, None,
                                  ALU.bitwise_and).then_inc(x_power_made, 1)
                dve.wait_ge(x_power_made, m + 1)
                dve.tensor_scalar(x_magic[:, u, :].bitcast(F32), x_magic[:, u, :].bitcast(F32),
                                  NORMAL_MIN, 1.5 * SHIFT, ALU.max, ALU.mult).then_inc(x_magic_made, 1)
            if b:
                m = n + 1
                dve.wait_ge(silu_made, m * 2 + 2)
                dve.tensor_tensor(up[:, :], gate[:, :], up[:, :], ALU.mult).then_inc(t_made, 1)
                dve.wait_ge(t_made, m + 1)
                dve.tensor_reduce(t_max[:, v:v + 1], up[:, :], AX_X, ALU.max,
                                  apply_absolute_value=True).then_inc(t_max_made, 1)
                dve.wait_ge(t_max_made, m + 1)
                dve.tensor_scalar(t_scale[:, v:v + 1], t_max[:, v:v + 1], 1.0 / FP8_MAX, None,
                                  ALU.mult).then_inc(t_scale_made, 1)
                dve.wait_ge(t_scale_made, m + 1)
                dve.reciprocal(t_rscale[:, v:v + 1], t_scale[:, v:v + 1]).then_inc(t_rscale_made, 1)
            if b:
                dve.wait_ge(t_scaled_made, m + 1)
                if later(m, 1):
                    dve.wait_ge(t_rounded_made, m)
                dve.tensor_scalar(t_magic[:, :], t_scaled[:, :].bitcast(U32), 0x7F800000, None,
                                  ALU.bitwise_and).then_inc(t_power_made, 1)
                dve.wait_ge(t_power_made, m + 1)
                dve.tensor_scalar(t_magic[:, :].bitcast(F32), t_magic[:, :].bitcast(F32),
                                  NORMAL_MIN, 1.5 * SHIFT, ALU.max, ALU.mult).then_inc(t_magic_made, 1)
            if c:
                dve.wait_ge(down_made, n + 1)
                if later(n, 1):
                    dve.wait_ge(y_made, n)
                dve.scalar_tensor_tensor(out=y_down[:, :], in0=down[:, :], scalar=t_scale[:, u:u + 1],
                                         in1=srow[:, 2 * I_FF:2 * I_FF + D], op0=ALU.mult,
                                         op1=ALU.mult).then_inc(y_down_made, 1)

        dve.wait_ge(srow_in, 16)
        turns(dve, turn)

    @block.tensor
    def _(pe):
        def turn(n, u, a, b, c):
            v = 1 - u
            if a:
                m = n + 2
                pe.wait_ge(attn_lo, m + 1)
                if later(m, 1):
                    pe.wait_ge(h2_made, m)
                for j, (ap, wp) in enumerate([(0, 0), (0, 1), (1, 0)]):
                    for k in range(KC):
                        mm = pe.matmul(proj[:, :], attn[u][ap][:, k, :], woT[:, wp, k, :],
                                       start=(j == 0 and k == 0), stop=(j == 2 and k == KC - 1))
                mm.then_inc(proj_made, 1)
            if b:
                m = n + 1
                pe.wait_ge(x_rounded_made, m + 1)
                if later(m, 2):
                    pe.wait_ge(y_down_made, m - 1)
                for k in range(KC):
                    mm = pe.transpose(x_turned[:, k * P:(k + 1) * P], x_rounded[:, v, k * P:(k + 1) * P],
                                      identb[:, :])
                mm.then_inc(x_turned_made, 1)
                pe.wait_ge(xT_made, m + 1)
                for k in range(NGC):
                    if later(m, 1) or k >= 2:
                        pe.wait_ge(gu_used, m * NGC + k - 1)
                    for y_, col in ((0, 0), (1, I_FF)):
                        for kc in range(KC):
                            mm = pe.matmul(gu[2 * (k % 2) + y_][:, 0:GC], xT[v][:, kc, :],
                                           wguT[:, kc, col + k * GC:col + (k + 1) * GC],
                                           start=(kc == 0), stop=(kc == KC - 1))
                    mm.then_inc(gu_made, 1)
            if c:
                pe.wait_ge(t_rounded_made, n + 1)
                if later(n, 1):
                    pe.wait_ge(tT_made, n)
                for k in range(NI):
                    mm = pe.transpose(t_turned[:, k * P:(k + 1) * P], t_rounded[:, k * P:(k + 1) * P],
                                      identb[:, :])
                mm.then_inc(t_turned_made, 1)
            if c:
                pe.wait_ge(tT_made, n + 1)
                if later(n, 1):
                    pe.wait_ge(y_down_made, n)
                if not b:
                    pe.wait_ge(xT_made, NT)
                for k in range(NI):
                    mm = pe.matmul(down[:, :], tT[:, k, :], wdT[:, k, :], start=(k == 0),
                                   stop=(k == NI - 1))
                mm.then_inc(down_made, 1)

        for s in (woT_in, wguT_in, wdT_in):
            pe.wait_ge(s, 16)
        turns(pe, turn)


_INS = ["x", "L0_tok_weight", "L0_tok_lora_A", "L0_tok_lora_B", "L0_attn_W_qkv", "L0_attn_W_out",
        "L0_ffn_w_gate", "L0_ffn_w_up", "L0_ffn_w_down", "L0_ffn_up_reorder_index",
        "L0_ffn_down_reorder_index"]


def kernel(**inputs):
    import numpy as _np
    import concourse.bacc as _bacc
    from concourse import mybir as _mybir
    from concourse.bass_utils import run_bass_kernel_spmd as _run

    nc = _bacc.Bacc("TRN2", target_bir_lowering=False, num_devices=1)
    arrays, args = {}, []
    for name in _INS:
        a = _np.ascontiguousarray(inputs[name])
        arrays[f"in_{name}_dram"] = a
        args.append(nc.dram_tensor(f"in_{name}_dram", a.shape, _mybir.dt.from_np(a.dtype),
                                   kind="ExternalInput").ap())
    out = nc.dram_tensor("out_dram", (B, S, D), _mybir.dt.float32, kind="ExternalOutput").ap()
    build(nc, *args, out)
    r = _run(nc, [arrays], core_ids=[0])
    return r.results[0]["out_dram"]
```

```python
from contextlib import ExitStack

import concourse.bass as bass
from concourse import mybir

ds = bass.ds
ALU = mybir.AluOpType
ACT = mybir.ActivationFunctionType
AX_X = mybir.AxisListType.X
F32 = mybir.dt.float32
F32R = mybir.dt.float32r
BF16 = mybir.dt.bfloat16
I32 = mybir.dt.int32
U32 = mybir.dt.uint32

P = 128
B, S = 2, 1024
D = 512
KC = D // P
NT = B * S // P
H, HD = 16, 32
GH = P // HD
G = H // GH
RANK = 16
LORA_SCALING = 2.0
I_FF = 1408
NI = I_FF // P
NF = KC + 2 * NI
GC = 352
NGC = I_FF // GC
QT = S // P
C = 512
NC = S // C
EPS = 1e-5
FP8_MAX = 448.0
MASKED = -1.0e30
SM_SCALE = float(HD) ** -0.5
NORMAL_MIN = 2.0 ** -6
SHIFT = 2.0 ** 20


def build(nc, x, tok_w, lora_a, lora_b, w_qkv, w_out, w_gate, w_up, w_down, up_idx, down_idx, out):
    h_dram = nc.dram_tensor("h_scratch", (NT, P, D), F32, kind="Internal").ap()
    attnT_dram = nc.dram_tensor("attnT_scratch", (G, P, B * S), F32, kind="Internal").ap()
    wguT_dram = nc.dram_tensor("wguT_scratch", (P, KC, 2 * I_FF), BF16, kind="Internal").ap()
    wdT_dram = nc.dram_tensor("wdT_scratch", (I_FF, D), BF16, kind="Internal").ap()
    wscale_dram = nc.dram_tensor("wscale_scratch", (1, NF * P), F32, kind="Internal").ap()

    with ExitStack() as top:
        identf = top.enter_context(nc.sbuf_tensor("identf", [P, P], F32))
        identb = top.enter_context(nc.sbuf_tensor("identb", [P, P], BF16))
        onesf = top.enter_context(nc.sbuf_tensor("onesf", [P, HD], F32))
        xT = top.enter_context(nc.sbuf_tensor("xT", [P, 2, KC, B * S], F32R))
        w_rows = top.enter_context(nc.sbuf_tensor("w_rows", [P, KC, D], F32))
        flat = xT[:, :, :, :].rearrange("p a k n -> p (a k n)").bitcast(F32)
        ends = [0]
        for words in (KC * I_FF, NI * D // 2, NF * P):
            ends.append(ends[-1] + words)
        wguT, wdT, srow = (flat[:, i:j] for i, j in zip(ends, ends[1:]))
        feed_weights = (wguT.bitcast(BF16).rearrange("p (k n) -> p k n", k=KC),
                        wdT.bitcast(BF16).rearrange("p (k n) -> p k n", k=NI),
                        srow, w_rows[:, :, :])
        w_qkv_groups = w_qkv.rearrange("(y g p) n -> y g p n", y=3, p=P)
        with ExitStack() as ctx:
            prepare(nc, ctx, identf, identb, onesf, xT, w_rows, w_qkv_groups, x, tok_w, lora_a,
                    lora_b, w_gate, w_up, w_down, down_idx, h_dram, wguT_dram, wdT_dram, wscale_dram)
        with ExitStack() as ctx:
            attend(nc, ctx, identf, identb, onesf, xT,
                   w_rows, w_qkv_groups, attnT_dram, feed_weights,
                   (wguT_dram, wdT_dram.rearrange("(k p) n -> p k n", p=P), wscale_dram.to_broadcast([P, NF * P]),
                    w_out.rearrange("(t p) n -> p t n", p=P)))
        with ExitStack() as ctx:
            feed(nc, ctx, identf, identb, feed_weights, h_dram, attnT_dram, out)


def allocators(nc, ctx, block):
    def sb(name, shape, dt=F32):
        return ctx.enter_context(nc.sbuf_tensor(f"{block}_{name}", shape, dt))

    def ps(name, shape, dt=F32):
        return ctx.enter_context(nc.psum_tensor(f"{block}_{name}", shape, dt))

    def sem(name):
        return ctx.enter_context(nc.semaphore(f"{block}_{name}"))

    return sb, ps, sem


def later(n, k):
    return not isinstance(n, int) or n >= k


def prepare(nc, ctx, identf, identb, onesf, xT, w_rows, w_qkv, x, tok_w, lora_a, lora_b, w_gate,
            w_up, w_down, down_idx, h_dram, wguT_dram, wdT_dram, wscale_dram):
    sb, ps, sem = allocators(nc, ctx, "prep")
    SLOTS = 4
    AHEAD = 2
    EARLY = 8
    didx = sb("didx", [P, NI], I32)
    gu_rows = sb("gu_rows", [P, SLOTS, D])
    down_rows = sb("down_rows", [P, KC, I_FF])
    scaled = sb("scaled", [P, 2, I_FF])
    magic = sb("magic", [P, 2, I_FF], U32)
    rounded = sb("rounded", [P, 2, I_FF], BF16)
    row_max = sb("row_max", [P, 2])
    row_scale = sb("row_scale", [P, 2])
    all_scales = sb("all_scales", [P, NF])
    row_rscale = sb("row_rscale", [P, 2])
    scale_rows = sb("scale_rows", [NF, P])
    wguT = sb("wguT", [P, KC, 2 * I_FF], BF16)
    wdT = sb("wdT", [P, NI, D], BF16)
    tok_ids = sb("tok_ids", [P, NT], I32)
    emb = sb("emb", [P, 2, D])
    lrow = sb("lrow", [P, 2, RANK])
    lrowT = sb("lrowT", [RANK, 2, P])
    lb = sb("lb", [RANK, D])
    hid = sb("hid", [P, 2, D])
    stats = sb("stats", [P, 2, 6])
    mean_var = sb("mean_var", [P, 2, 2])
    var_eps = sb("var_eps", [P, 2])
    rstd = sb("rstd", [P, 2])
    minus_half = sb("minus_half", [P, 1])
    eps = sb("eps", [P, 1])
    xn = sb("xn", [P, 2, D])
    wturned = [ps(f"wturned{u}", [P, 2048], BF16) for u in range(2)]
    turned = [ps(f"turned{u}", [P, D]) for u in range(2)]
    lora = ps("lora", [P, D])
    lturned = ps("lturned", [P, D])

    idx_in = sem("idx_in")
    gu_in = [sem(f"gu_in{k}") for k in range(SLOTS)]
    down_in = [sem(f"down_in{n}") for n in range(KC)]
    ident_made = sem("ident_made")
    row_max_made = sem("row_max_made")
    row_scale_made = sem("row_scale_made")
    row_rscale_made = sem("row_rscale_made")
    scale_kept = sem("scale_kept")
    scaled_made = sem("scaled_made")
    power_made = sem("power_made")
    magic_made = sem("magic_made")
    sum_made = sem("sum_made")
    rounded_made = sem("rounded_made")
    wturned_made = sem("wturned_made")
    wturned_used = sem("wturned_used")
    scales_turned = sem("scales_turned")
    scale_rows_made = sem("scale_rows_made")
    w_stored = sem("w_stored")
    w_rows_in = sem("w_rows_in")
    wd_stored = sem("wd_stored")
    ids_in = sem("ids_in")
    lb_in = sem("lb_in")
    emb_in = [sem(f"emb_in{u}") for u in range(2)]
    l_turned = sem("l_turned")
    l_copied = sem("l_copied")
    l_mm = sem("l_mm")
    h_made = sem("h_made")
    stats_made = sem("stats_made")
    mean_made = sem("mean_made")
    half_made = sem("half_made")
    var_made = sem("var_made")
    rstd_made = sem("rstd_made")
    xn_made = sem("xn_made")
    x_turned = sem("x_turned")
    x_hi = sem("x_hi")
    x_lo = sem("x_lo")
    h_stored = [sem(f"h_stored{u}") for u in range(2)]

    block = ctx.enter_context(nc.Block())

    def steps(eng, step):
        for n in range(KC):
            step(n, n, n, n % 2)

        def four(t):
            for k in range(4):
                step(t * 4 + KC + k, k, t * 2 + KC + k // 2 if k % 2 == 0 else None, k // 2)

        four(0)
        with eng.Fori(1, LOOPS) as t:
            four(t)
        for j in range(NF - KC - 4 * LOOPS):
            m = KC + 2 * LOOPS + j
            step(KC + 4 * LOOPS + j, j % 4, m, m % 2)

    LOOPS = 5
    assert KC + 2 * LOOPS + NF - KC - 4 * LOOPS == NT and KC % 4 == 0

    def rows(n, k):
        if isinstance(n, int) and n < KC:
            return down_rows[:, n, :], I_FF
        return gu_rows[:, k, :], D

    def in_flight(m, v):
        return (m - v) * 16 + 32

    def x_part(part, m):
        return xT[:, part, :, ds(m * P, P)]

    @block.sync
    def _(sp):
        sp.dma_start(tok_ids[:, :].rearrange("p (b t) -> p b t", b=B),
                     x.rearrange("b (t p) -> p b t", p=P), allow_slow_non_contiguous=True
                     ).then_inc(ids_in, 16)
        sp.dma_start(lb[:, :], lora_b[:, :]).then_inc(lb_in, 16)
        for n in range(KC):
            if n == 1:
                sp.wait_ge(emb_in[0], in_flight(0, 0))
            sp.dma_start(down_rows[:, n, :], w_down[n * P:(n + 1) * P, :]).then_inc(down_in[n], 16)
        sp.dma_start(didx[:, :], down_idx.rearrange("(t p) -> p t", p=P), allow_slow_non_contiguous=True
                     ).then_inc(idx_in, 16)

        def load_rows(n, k):
            if later(n, KC + SLOTS):
                sp.wait_ge(scaled_made, n - SLOTS + 1)
            row = (n - KC - k % 2) * (P // 2)
            sp.dma_start(gu_rows[:, k, :], (w_gate, w_up)[k % 2][ds(row, P), :]).then_inc(gu_in[k], 16)

        for n in range(KC, KC + AHEAD):
            load_rows(n, n - KC)

        def step(n, k, m, v):
            if not isinstance(n, int) or KC <= n < NF - AHEAD:
                load_rows(n + AHEAD, (k + AHEAD) % SLOTS)
            if isinstance(n, int) and n == NF - 2:
                sp.wait_ge(wturned_used, KC + 2 * EARLY)
                store_columns(0, EARLY)
            if m is not None:
                sp.wait_ge(h_made, m + 1)
                sp.dma_start(h_dram[ds(m, 1), :, :].rearrange("a p n -> p (a n)"), hid[:, v, :]
                             ).then_inc(h_stored[v], 16)

        def store_columns(begin, end):
            to, source = (w[:, :, :].rearrange("p k (y n) -> p (k y) n", y=2)[:, :, begin * P:end * P]
                          for w in (wguT_dram, wguT))
            sp.dma_start(to, source).then_inc(w_stored, 16)

        steps(sp, step)
        sp.dma_start(w_rows[:, 0:3, :], w_qkv[:, 0, :, :].rearrange("y p n -> p y n")).then_inc(w_rows_in, 16)
        sp.wait_ge(scale_rows_made, 1)
        sp.dma_start(wscale_dram.rearrange("a (n p) -> (a n) p", p=P), scale_rows[:, :]
                     ).then_inc(w_stored, 16)
        sp.wait_ge(wturned_used, NF)
        store_columns(EARLY, NI)
        sp.wait_ge(w_rows_in, 16)
        sp.wait_ge(w_stored, 48)
        for u in range(2):
            sp.wait_ge(h_stored[u], 16 * NT // 2)

    @block.gpsimd
    def _(pool):
        pool.memset(identf[:, :], 0.0).then_inc(ident_made, 1)
        pool.memset(onesf[:, :], 1.0).then_inc(ident_made, 1)
        pool.memset(minus_half[:, :], -0.5).then_inc(half_made, 1)
        pool.memset(eps[:, :], EPS).then_inc(half_made, 1)
        pool.wait_ge(ident_made, 2)
        pool.affine_select(out=identf[:, :], in_=identf[:, :], compare_op=ALU.not_equal, fill=1.0,
                           base=0, pattern=[[-1, P]], channel_multiplier=1).then_inc(ident_made, 1)
        pool.wait_ge(ident_made, 3)
        pool.tensor_copy(identb[:, :], identf[:, :]).then_inc(ident_made, 1)
        pool.wait_ge(half_made, 2)

        def scatter_down(r):
            pool.wait_ge(idx_in, 16)
            pool.wait_ge(wturned_used, KC)
            pool.indirect_dma_start(
                out=wdT_dram, out_offset=bass.IndirectOffsetOnAxis(ap=didx[:, r:r + 1], axis=0),
                in_=wdT[:, r, :], in_offset=None,
            ).then_inc(wd_stored, 16)

        def gather_token(m, v):
            if m >= 2:
                pool.wait_ge(h_made, m - 1)
                pool.wait_ge(l_turned, m - 1)
            for rows, table in ((emb, tok_w), (lrow, lora_a)):
                pool.indirect_dma_start(
                    out=rows[:, v, :], out_offset=None, in_=table,
                    in_offset=bass.IndirectOffsetOnAxis(ap=tok_ids[:, m:m + 1], axis=0),
                ).then_inc(emb_in[v], 16)

        def make_rstd(m, v):
            pool.wait_ge(mean_made, m + 1)
            pool.tensor_tensor(var_eps[:, v:v + 1], mean_var[:, v, 1:2], eps[:, :], ALU.add
                               ).then_inc(var_made, 1)
            pool.wait_ge(var_made, m + 1)
            pool.tensor_tensor(rstd[:, v:v + 1], var_eps[:, v:v + 1], minus_half[:, :], ALU.pow
                               ).then_inc(rstd_made, 1)

        def round_tile(n, u):
            _, N = rows(n, 0)
            pool.wait_ge(sum_made, n + 1)
            if n >= 2:
                pool.wait_ge(wturned_made, n - 1)
            pool.tensor_tensor(rounded[:, u, 0:N], scaled[:, u, 0:N],
                               magic[:, u, 0:N].bitcast(F32), ALU.subtract).then_inc(rounded_made, 1)

        pool.wait_ge(ids_in, 16)
        gather_token(0, 0)
        gather_token(1, 1)
        tokens = {}
        for n in range(NF):
            if n < KC or n >= KC + 4 * LOOPS:
                tokens[n] = n if n < KC else n - 2 * LOOPS
            elif (n - KC) % 2 == 0:
                tokens[n] = KC + (n - KC) // 2
        for n in range(NF):
            if n in tokens:
                m = tokens[n]
                make_rstd(m, m % 2)
                if m + 2 < NT:
                    gather_token(m + 2, m % 2)
            if n >= 1:
                round_tile(n - 1, (n - 1) % 2)
            if 0 <= n - 2 * KC < NI:
                scatter_down(n - 2 * KC)
        round_tile(NF - 1, (NF - 1) % 2)
        pool.wait_ge(wd_stored, 16 * NI)

    @block.vector
    def _(dve):
        def scale_tile(n, k):
            src, N = rows(n, k)
            u = k % 2
            if isinstance(n, int) and n < KC:
                dve.wait_ge(down_in[n], 16)
            else:
                dve.wait_ge(gu_in[k], (n - k - KC) * 4 + 16)
            if later(n, 2):
                dve.wait_ge(row_scale_made, n - 1)
            dve.tensor_reduce(row_max[:, u:u + 1], src, AX_X, ALU.max,
                              apply_absolute_value=True).then_inc(row_max_made, 1)
            dve.wait_ge(row_max_made, n + 1)
            if later(n, 2):
                dve.wait_ge(scale_kept, n - 1)
            dve.tensor_scalar(row_scale[:, u:u + 1], row_max[:, u:u + 1], 1.0 / FP8_MAX, None,
                              ALU.mult).then_inc(row_scale_made, 1)
            dve.wait_ge(row_scale_made, n + 1)
            if later(n, 2):
                dve.wait_ge(scaled_made, n - 1)
            dve.reciprocal(row_rscale[:, u:u + 1], row_scale[:, u:u + 1]).then_inc(row_rscale_made, 1)

        def magic_tile(n, u):
            _, N = rows(n, 0)
            dve.wait_ge(scaled_made, n + 1)
            if later(n, 2):
                dve.wait_ge(rounded_made, n - 1)
            dve.tensor_scalar(magic[:, u, 0:N], scaled[:, u, 0:N].bitcast(U32), 0x7F800000, None,
                              ALU.bitwise_and).then_inc(power_made, 1)
            dve.wait_ge(power_made, n + 1)
            dve.tensor_scalar(magic[:, u, 0:N].bitcast(F32), magic[:, u, 0:N].bitcast(F32),
                              NORMAL_MIN, 1.5 * SHIFT, ALU.max, ALU.mult).then_inc(magic_made, 1)
            dve.wait_ge(magic_made, n + 1)
            dve.tensor_tensor(scaled[:, u, 0:N], scaled[:, u, 0:N], magic[:, u, 0:N].bitcast(F32),
                              ALU.add).then_inc(sum_made, 1)

        def hidden(m, v):
            dve.wait_ge(l_mm, m + 1)
            dve.wait_ge(emb_in[v], in_flight(m, v))
            if later(m, 2):
                dve.wait_ge(h_stored[v], (m - v) * 8)
            dve.scalar_tensor_tensor(out=hid[:, v, :], in0=lora[:, :], scalar=LORA_SCALING,
                                     in1=emb[:, v, :], op0=ALU.mult, op1=ALU.add).then_inc(h_made, 1)
            dve.wait_ge(h_made, m + 1)
            dve.bn_stats(stats[:, v, :], hid[:, v, :]).then_inc(stats_made, 1)
            dve.wait_ge(stats_made, m + 1)

        def aggregate(m, v):
            dve.bn_aggr(mean_var[:, v, :], stats[:, v, :]).then_inc(mean_made, 1)

        def normal(m, v):
            dve.wait_ge(rstd_made, m + 1)
            if later(m, 2):
                dve.wait_ge(x_turned, m - 1)
            dve.tensor_scalar(xn[:, v, :], hid[:, v, :], mean_var[:, v, 0:1], rstd[:, v:v + 1],
                              ALU.subtract, ALU.mult).then_inc(xn_made, 1)

        def low(m, v):
            dve.wait_ge(x_hi, m + 1)
            dve.tensor_tensor(x_part(1, m), turned[v][:, :].rearrange("p (k c) -> p k c", c=P),
                              x_part(0, m).bitcast(F32), ALU.subtract).then_inc(x_lo, 1)

        def step(n, k, m, v):
            if m is not None:
                hidden(m, v)
            scale_tile(n, k)
            if m is not None:
                aggregate(m, v)
            if later(n, 1):
                magic_tile(n - 1, (k - 1) % 2)
            if m is not None:
                if later(m, 2):
                    low(m - 2, v)
                normal(m, v)

        dve.wait_ge(ident_made, 4)
        steps(dve, step)
        magic_tile(NF - 1, (NF - 1) % 2)
        low(NT - 2, 0)
        low(NT - 1, 1)

    @block.scalar
    def _(act):
        def scaled_tile(n, k):
            src, N = rows(n, k)
            act.wait_ge(row_scale_made, n + 1)
            if isinstance(n, int):
                col = n if n < KC else KC + (n - KC) // 2 + (n - KC) % 2 * NI
                at = slice(col, col + 1)
            else:
                at = ds((n + KC) // 2 if k % 2 == 0 else (n + KC - 1) // 2 + NI, 1)
            act.activation(all_scales[:, at], row_scale[:, k % 2:k % 2 + 1], ACT.Copy
                           ).then_inc(scale_kept, 1)
            act.wait_ge(row_rscale_made, n + 1)
            if later(n, 2):
                act.wait_ge(rounded_made, n - 1)
            act.activation(scaled[:, k % 2, 0:N], src, ACT.Copy, scale=row_rscale[:, k % 2:k % 2 + 1]
                           ).then_inc(scaled_made, 1)

        def keep_tile(n, u):
            act.wait_ge(wturned_made, n + 1)
            if isinstance(n, int) and n < KC:
                to, N = wdT[:, :, n * P:(n + 1) * P], I_FF
            else:
                to, N = wguT[:, :, ds((n - KC - u) * (P // 2) + u * I_FF, P)], D
            act.activation(to, wturned[u][:, 0:N].rearrange("p (k c) -> p k c", c=P),
                           ACT.Copy).then_inc(wturned_used, 1)

        def copy_l(m, v):
            act.wait_ge(l_turned, m + 1)
            if later(m, 2):
                act.wait_ge(l_mm, m - 1)
            act.activation(lrowT[:, v, :], lturned[0:RANK, 0:P], ACT.Copy).then_inc(l_copied, 1)

        def high(m, v):
            act.wait_ge(x_turned, m + 1)
            act.activation(x_part(0, m), turned[v][:, :].rearrange("p (k c) -> p k c", c=P),
                           ACT.Copy).then_inc(x_hi, 1)

        def step(n, k, m, v):
            scaled_tile(n, k)
            if m is not None and (not isinstance(m, int) or m + 1 < NT):
                copy_l(m + 1, 1 - v)
            if m is not None and later(m, 1):
                high(m - 1, 1 - v)
            if later(n, 2):
                keep_tile(n - 2, k % 2)

        copy_l(0, 0)
        steps(act, step)
        act.wait_ge(scales_turned, 1)
        act.activation(scale_rows[:, :], lturned[0:NF, 0:P], ACT.Copy).then_inc(scale_rows_made, 1)
        high(NT - 1, 1)
        for n in range(NF - 2, NF):
            keep_tile(n, n % 2)

    @block.tensor
    def _(pe):
        def turn_ffn(n, u):
            _, N = rows(n, 0)
            pe.wait_ge(rounded_made, n + 1)
            if later(n, 2):
                pe.wait_ge(wturned_used, n - 1)
            for k in range(N // P):
                mm = pe.transpose(wturned[u][:, k * P:(k + 1) * P], rounded[:, u, k * P:(k + 1) * P],
                                  identb[:, :])
            mm.then_inc(wturned_made, 1)

        def lora_tile(m, v):
            pe.wait_ge(emb_in[v], in_flight(m, v))
            if later(m, 1):
                pe.wait_ge(l_copied, m)
            pe.transpose(lturned[0:RANK, 0:P], lrow[:, v, :], identf[:, :]).then_inc(l_turned, 1)
            pe.wait_ge(l_copied, m + 1)
            if later(m, 1):
                pe.wait_ge(h_made, m)
            pe.matmul(lora[:, :], lrowT[:, v, :], lb[:, :], start=True, stop=True).then_inc(l_mm, 1)

        def turn_token(m, v):
            pe.wait_ge(xn_made, m + 1)
            if later(m, 2):
                pe.wait_ge(x_lo, m - 1)
            for c in range(KC):
                mm = pe.transpose(turned[v][:, c * P:(c + 1) * P], xn[:, v, c * P:(c + 1) * P],
                                  identf[:, :])
            mm.then_inc(x_turned, 1)

        def step(n, k, m, v):
            if m is not None:
                if not isinstance(m, int) or m + 1 < NT:
                    lora_tile(m + 1, 1 - v)
                if later(m, 1):
                    turn_token(m - 1, 1 - v)
            if later(n, 2):
                turn_ffn(n - 2, k % 2)

        pe.wait_ge(lb_in, 16)
        pe.wait_ge(ident_made, 4)
        lora_tile(0, 0)
        steps(pe, step)
        pe.wait_ge(l_copied, NT)
        pe.wait_ge(scale_kept, NF)
        pe.transpose(lturned[0:NF, 0:P], all_scales[:, :], identf[:, :]).then_inc(scales_turned, 1)
        turn_token(NT - 1, 1)
        for n in range(NF - 2, NF):
            turn_ffn(n, n % 2)


def attend(nc, ctx, identf, identb, onesf, xT, w_rows, w_qkv, attnT_dram, feed_weights,
           feed_sources):
    sb, ps, sem = allocators(nc, ctx, "attn")
    w = sb("w", [P, 3, 2, KC, P], F32R)
    qk = sb("qk", [P, 2, 2, S], F32R)
    vT = sb("vT", [P, S])
    q_stack = [sb(f"q_stack{u}", [P, GH, S], F32R) for u in range(2)]
    k_stack = [sb(f"k_stack{u}", [P, GH, S], F32R) for u in range(2)]
    v = [sb(f"v{u}", [P, QT, P]) for u in range(2)]
    probs = sb("probs", [P, 2, GH, C])
    part_max = sb("part_max", [P, 2, GH, QT])
    neg_max = sb("neg_max", [P, GH, QT])
    neg_max_parts = sb("neg_max_parts", [P, 2, GH, QT])
    max_rows = sb("max_rows", [2 * GH * QT, P])
    out_copy = sb("out_copy", [P, C])
    denom_copy = sb("denom_copy", [P, C])
    rdenom = sb("rdenom", [P, C])
    attnT = sb("attnT", [P, 2, C])
    go = sb("go", [P, 1])
    mask_keys = sb("mask_keys", [P, P], BF16)
    mask_queries = sb("mask_queries", [P, P], BF16)

    scoresT = [ps(f"scoresT{u}", [P, 2, C]) for u in range(2)]
    outT = ps("outT", [P, C])
    denom = ps("denom", [P, C])
    work = [ps(f"work{u}", [P, C]) for u in range(2)]

    masks_made = sem("masks_made")
    w_in = sem("w_in")
    w_hi = sem("w_hi")
    work_made = sem("work_made")
    work_free = [sem(f"work_free{u}") for u in range(2)]
    qk_hi = sem("qk_hi")
    stack_in = [[sem(f"{y}_stack_in{u}") for y in ("q", "k", "k_pool")] for u in range(2)]
    go_made = sem("go_made")
    part_max_made = sem("part_max_made")
    neg_max_made = sem("neg_max_made")
    max_rows_in = [sem(f"max_rows_in{u}") for u in range(2)]
    scoresT_made = sem("scoresT_made")
    probs_made = sem("probs_made")
    probs_used = sem("probs_used")
    out_copied = sem("out_copied")
    rdenom_made = sem("rdenom_made")
    attn_made = sem("attn_made")
    feed_weights_in = sem("feed_weights_in")
    attn_stored = [sem(f"attn_stored{u}") for u in range(2)]

    STACKED = [("q", (0, 1, 2)), ("k", (0,)), ("k", (1, 2))]
    RQ = 4
    Q_SLOTS = [0, 1]
    V_SLOTS = [6, 9, 12, 14]
    FIRST_SCORES = 19
    STEPS = [(c, j, max(c * C, j * P), (c + 1) * C - max(c * C, j * P))
             for c in range(NC) for j in range((c + 1) * C // P)]
    NS = len(STEPS)
    SCORES = [(h, t, k0, min(C, (t + 1) * P - k0)) for h in range(GH) for t in range(QT)
              for k0 in range(0, (t + 1) * P, C)]
    MAKE_V = [(y, c) for y in ("k", "q", "v", "vt") for c in range(NC)]
    MAKE_MAX = [("s", n) for n in range(len(SCORES))] + [("m", a) for a in range(2)]
    WEIGHTS = [("w", c) for c in range(KC)]
    NW = len(WEIGHTS)
    NP = len(MAKE_V) + len(MAKE_MAX)
    assert NP % 2 == 0 and NW % 2 == 0
    NSC = len(SCORES)
    SLOTS = 4
    FIRST = MAKE_V[:NC]

    def slots(weights):
        at = [[] for _ in range(NS * SLOTS)]
        for slot, piece in zip(Q_SLOTS + V_SLOTS, MAKE_V[NC:]):
            at[slot].append(piece)
        if weights:
            for n, piece in enumerate(WEIGHTS):
                at[V_SLOTS[-1] + 1 + n].append(piece)
        for n in range(NSC):
            at[FIRST_SCORES + n * (NS * SLOTS - 2 - FIRST_SCORES) // NSC].append(("s", n))
        at[-1] += MAKE_MAX[NSC:]
        return at

    AT = {weights: slots(weights) for weights in (False, True)}
    NUMBER = {weights: {piece: n for n, piece in enumerate(FIRST + sum(AT[weights], []))}
              for weights in AT}

    def number(i, b, piece):
        return NUMBER[b == 1 and not (isinstance(i, int) and i == 2 * G - 1)][piece]

    def ends_chunk(s, slot):
        if s == NS:
            return NC - 1
        if slot == 0 and s >= 2 and STEPS[s - 1][0] == STEPS[s - 2][0] + 1:
            return STEPS[s - 2][0]
        return None

    block = ctx.enter_context(nc.Block())

    def stacked(i, b, k):
        return (i - b) * (8 * GH * len(STACKED[k][1])) + 16 * GH * len(STACKED[k][1])

    def turns(eng, prepare, attend_slot):
        def half(ia, ip, weights=False):
            n = len(FIRST)
            if ip is not None:
                for k, piece in enumerate(FIRST):
                    prepare(*ip, piece, k)
            for slot in range(NS * SLOTS):
                if ia is not None:
                    attend_slot(*ia, slot // SLOTS, slot % SLOTS)
                if ip is not None:
                    for piece in AT[weights][slot]:
                        prepare(*ip, piece, n)
                        n += 1
            if ia is not None:
                attend_slot(*ia, NS, 0)
        for k, piece in enumerate(WEIGHTS):
            prepare(0, 0, -1, piece, k - NW)
        half(None, (0, 0, 0))
        half((0, 0, 0), (1, 1, 0), weights=True)
        half((1, 1, 0), (2, 0, 1))
        with eng.Fori(1, G - 1) as g:
            half((g * 2, 0, g), (g * 2 + 1, 1, g), weights=True)
            half((g * 2 + 1, 1, g), (g * 2 + 2, 0, g + 1))
        half((2 * G - 2, 0, G - 1), (2 * G - 1, 1, G - 1))
        half((2 * G - 1, 1, G - 1), None)

    def pieces(i, b, n):
        return (i - b) * (NP + NW // 2) + b * NP + NW + n

    def in_bank(i, b, n):
        return (i - b) * ((NP + NW // 2) // 2) + (b * NP + NW + n) // 2


    def stack_waits(eng, i, b, n):
        eng.wait_ge(work_free[1 - n % 2], in_bank(i, b, n - 1) + 1)
        if later(i, 2):
            eng.wait_ge(scoresT_made, (i - 1) * 2 * NS)
        eng.wait_ge(work_free[n % 2], in_bank(i, b, n) + 1)

    def stack(eng, b, which):
        kind, blocks = STACKED[which]
        y = "qk".index(kind)
        to = (q_stack, k_stack)[y][b]
        parts = ((0, 0, 1), (0, 1, 0))[y]
        for r in blocks:
            for h in range(GH):
                eng.dma_start(to[r * HD:(r + 1) * HD, h, :].bitcast(F32),
                              qk[h * HD:(h + 1) * HD, y, parts[r], :].bitcast(F32)
                              ).then_inc(stack_in[b][which], 16)

    @block.sync
    def _(sp):
        def load_w(g):
            sp.wait_ge(work_made, pieces((g - 1) * 2, 0, 0))
            sp.dma_start(w_rows[:, 0:3, :], w_qkv[:, ds(g, 1), :, :].rearrange("y g p n -> p (y g) n")
                         ).then_inc(w_in, 16)

        def prepare(i, b, g, piece, n):
            kind, c = piece
            u = n % 2
            if kind in "qk" and c == NC - 1:
                stack_waits(sp, i, b, n)
                stack(sp, b, "qk".index(kind))
            if kind == "vt" and c == 0 and isinstance(i, int) and i == 2 * G - 1:
                sp.wait_ge(work_made, pieces(i, b, n))
                for to, source in zip(feed_weights, feed_sources):
                    sp.dma_start(to, source).then_inc(feed_weights_in, 16)
            if kind == "q" and c == 0 and b == 1:
                if not isinstance(g, int) or g < G - 1:
                    load_w(g + 1)
            if kind == "m" and c == 1:
                sp.wait_ge(work_free[1 - u], in_bank(i, b, n - 1) + 1)
                sp.wait_ge(work_free[u], in_bank(i, b, n) + 1)
                for part in range(2):
                    sp.dma_start(q_stack[b][3 * HD + part:3 * HD + part + 1, :, :].bitcast(F32)
                                 .rearrange("a h (t q) -> a (h t) q", q=P),
                                 max_rows[part * GH * QT:(part + 1) * GH * QT, :]
                                 ).then_inc(max_rows_in[b], 16)

        def attend_slot(i, b, g, s, slot):
            c = ends_chunk(s, slot)
            if c is not None:
                sp.wait_ge(attn_made, i * NC + c + 1)
                sp.dma_start(attnT_dram[ds(g, 1), :, b * S + c * C:b * S + (c + 1) * C]
                             .rearrange("a p n -> p (a n)"), attnT[:, c, :]
                             ).then_inc(attn_stored[c], 16)

        turns(sp, prepare, attend_slot)
        sp.wait_ge(feed_weights_in, 16 * len(feed_weights))
        for c in range(NC):
            sp.wait_ge(attn_stored[c], 16 * 2 * G)

    @block.gpsimd
    def _(pool):
        for n, (out, value) in enumerate(
                [(mask_keys[:, :], 0.0), (mask_queries[:, :], 0.0), (part_max[:, 1, :, :], 3.0e38)]
                + [(k_stack[u][3 * HD:3 * HD + 2, :, :].bitcast(F32), 1.0) for u in range(2)]):
            pool.memset(out, value).then_inc(masks_made, 1)
            pool.wait_ge(masks_made, n + 1)
        pool.affine_select(out=mask_keys[:, :], in_=mask_keys[:, :], compare_op=ALU.is_ge,
                           fill=MASKED, base=0, pattern=[[-1, P]], channel_multiplier=1
                           ).then_inc(masks_made, 1)
        pool.wait_ge(masks_made, 6)
        pool.affine_select(out=mask_queries[:, :], in_=mask_queries[:, :], compare_op=ALU.is_ge,
                           fill=MASKED, base=0, pattern=[[1, P]], channel_multiplier=-1
                           ).then_inc(masks_made, 1)

        def prepare(i, b, g, piece, n):
            kind, c = piece
            if kind == "k" and c == NC - 1:
                if later(i, 1):
                    pool.wait_ge(go_made, i)
                stack_waits(pool, i, b, n)
                pool.tensor_tensor(go[:, :], onesf[:, 0:1], onesf[:, 0:1], ALU.mult
                                   ).then_inc(go_made, 1)
                stack(pool, b, 2)

        def attend_slot(i, b, g, s, slot):
            c = ends_chunk(s, slot)
            if c is not None:
                pool.wait_ge(rdenom_made, i * NC * RQ + (c + 1) * RQ)
                pool.wait_ge(out_copied, (i * NC + c) * 2 + 2)
                if later(i, 1):
                    pool.wait_ge(attn_stored[c], i * 16)
                pool.tensor_tensor(attnT[:, c, :], out_copy[:, :], rdenom[:, :], ALU.mult
                                   ).then_inc(attn_made, 1)

        turns(pool, prepare, attend_slot)

    @block.tensor
    def _(pe):
        def prepare(i, b, g, piece, n):
            kind, c = piece
            u = n % 2
            bank = work[u]
            if later(i, 1) or n >= 2 - NW:
                pe.wait_ge(work_free[u], in_bank(i, b, n))
            if kind in "qkv":
                y = "qkv".index(kind)
                if n == 0 and b == 0:
                    pe.wait_ge(work_free[1], in_bank(i, b, 0))
                terms = [(0, 0), (0, 1), (1, 0)]
                for m, (wp, xp) in enumerate(terms):
                    for kc in range(KC):
                        mm = pe.matmul(bank[:, :], w[:, y, wp, kc, :],
                                       xT[:, xp, kc, b * S + c * C:b * S + (c + 1) * C],
                                       start=(m == 0 and kc == 0), stop=(m == 2 and kc == KC - 1))
            elif kind == "w":
                if c == 0 and later(g, 0):
                    pe.wait_ge(w_in, g * 16 + 16)
                for y in range(3):
                    mm = pe.transpose(bank[:, y * P:(y + 1) * P], w_rows[:, y, c * P:(c + 1) * P],
                                      identf[:, :])
            elif kind == "vt":
                if c == 0:
                    for k in range(NC):
                        m = number(i, b, ("v", k))
                        pe.wait_ge(work_free[m % 2], in_bank(i, b, m) + 1)
                for t in range(4):
                    mm = pe.transpose(bank[:, t * P:(t + 1) * P], vT[:, (4 * c + t) * P:(4 * c + t + 1) * P],
                                      identf[:, :])
            elif kind == "s":
                h, t, k0, nk = SCORES[c]
                if c == 0:
                    if not later(i, 1):
                        pe.wait_ge(masks_made, 7)
                    for k in range(3):
                        pe.wait_ge(stack_in[b][k], stacked(i, b, k))
                diagonal = k0 + nk == (t + 1) * P
                mm = pe.matmul(bank[:, 0:nk], q_stack[b][0:3 * HD, h, t * P:(t + 1) * P],
                               k_stack[b][0:3 * HD, h, k0:k0 + nk], start=True, stop=not diagonal)
                if diagonal:
                    mm = pe.matmul(bank[:, nk - P:nk], identb[:, :], mask_keys[:, :],
                                   start=False, stop=True)
            else:
                pe.wait_ge(neg_max_made, i * 3 + 3)
                mm = pe.transpose(bank[0:GH * QT, 0:P], neg_max_parts[:, c, :, :].rearrange("p h t -> p (h t)"),
                                  identf[:, :])
            mm.then_inc(work_made, 1)

        def values(i, b, s, ones):
            c, j, q0, nq = STEPS[s]
            if not ones:
                if j == 0 and (later(i, 1) or c > 0):
                    pe.wait_ge(out_copied, (i * NC + c) * 2)
                if s == 0:
                    for n in range(2):
                        m = number(i, b, ("vt", n))
                        pe.wait_ge(work_free[m % 2], in_bank(i, b, m) + 1)
                pe.wait_ge(probs_made, i * 2 * NS + 2 * s + 2)
            for h in range(GH):
                mm = pe.matmul((denom if ones else outT)[h * HD:(h + 1) * HD, q0 - c * C:q0 - c * C + nq],
                               onesf[:, 0:HD] if ones else v[b][:, j, h * HD:(h + 1) * HD],
                               probs[:, s % 2, h, 0:nq], start=(j == 0),
                               stop=(j == (c + 1) * C // P - 1))
            if ones:
                mm.then_inc(probs_used, 1)

        def attend_slot(i, b, g, s, slot):
            if s == NS:
                values(i, b, NS - 1, False)
                values(i, b, NS - 1, True)
                return
            c, j, q0, nq = STEPS[s]
            if slot >= 2:
                if s >= 1:
                    values(i, b, s - 1, slot == 3)
                return
            hp = slot
            if s == 0 and hp == 0:
                pe.wait_ge(max_rows_in[b], (i - b) * 16 + 32)
            if later(i, 1) or s >= 1:
                pe.wait_ge(probs_made, i * 2 * NS + max(2 * s + hp - 1, 0))
            for h2 in range(2):
                h = hp * 2 + h2
                diagonal = j * P >= c * C
                mm = pe.matmul(scoresT[hp][:, h2, 0:nq], k_stack[b][0:3 * HD + 2, h, j * P:(j + 1) * P],
                               q_stack[b][0:3 * HD + 2, h, q0:q0 + nq], start=True, stop=not diagonal)
                if diagonal:
                    mm = pe.matmul(scoresT[hp][:, h2, 0:P], identb[:, :], mask_queries[:, :],
                                   start=False, stop=True)
            mm.then_inc(scoresT_made, 1)

        turns(pe, prepare, attend_slot)

    @block.scalar
    def _(act):
        def prepare(i, b, g, piece, n):
            kind, c = piece
            u = n % 2
            if kind in "qk":
                y = "qk".index(kind)
                act.wait_ge(work_made, pieces(i, b, n) + 1)
                if c == 0 and later(i, 1):
                    for k in ((0,), (1, 2))[y]:
                        act.wait_ge(stack_in[1 - b][k], stacked(i - 1, 1 - b, k))
                act.activation(qk[:, y, 0, c * C:(c + 1) * C], work[u][:, :], ACT.Copy).then_inc(qk_hi, 1)
            elif kind == "w":
                act.wait_ge(work_made, pieces(i, b, n) + 1)
                act.activation(w[:, :, 0, c, :], work[u][:, 0:3 * P].rearrange("p (y c) -> p y c", c=P),
                               ACT.Copy).then_inc(w_hi, 1)
            elif kind == "v":
                act.wait_ge(work_made, pieces(i, b, n) + 1)
                act.activation(vT[:, c * C:(c + 1) * C], work[u][:, :], ACT.Copy
                               ).then_inc(work_free[u], 1)
            elif kind == "vt":
                act.wait_ge(work_made, pieces(i, b, n) + 1)
                act.activation(v[b][:, 4 * c:4 * c + 4, :],
                               work[u][:, :].rearrange("p (t d) -> p t d", d=P), ACT.Copy
                               ).then_inc(work_free[u], 1)

        def attend_slot(i, b, g, s, slot):
            if s < NS and slot < 2:
                c, j, q0, nq = STEPS[s]
                hp = slot
                act.wait_ge(scoresT_made, i * 2 * NS + 2 * s + hp + 1)
                if later(i, 1) or s >= 2:
                    act.wait_ge(probs_used, i * NS + max(s - 1, 0))
                act.activation(probs[:, s % 2, hp * 2:hp * 2 + 2, 0:nq], scoresT[hp][:, :, 0:nq],
                               ACT.Exp, scale=SM_SCALE).then_inc(probs_made, 1)
            c = ends_chunk(s, slot)
            if c is not None:
                end = NS if s == NS else s - 1
                act.wait_ge(probs_used, i * NS + end)
                if later(i, 1) or c > 0:
                    act.wait_ge(rdenom_made, (i * NC + c) * RQ)
                act.activation(denom_copy[:, :], denom[:, :], ACT.Copy).then_inc(out_copied, 1)
                if later(i, 1) or c > 0:
                    act.wait_ge(attn_made, i * NC + c)
                act.activation(out_copy[:, :], outT[:, :], ACT.Copy).then_inc(out_copied, 1)

        turns(act, prepare, attend_slot)

    @block.vector
    def _(dve):
        def prepare(i, b, g, piece, n):
            kind, c = piece
            u = n % 2
            if kind in "qk":
                y = "qk".index(kind)
                dve.wait_ge(qk_hi, i * 4 + n + 1)
                dve.tensor_tensor(qk[:, y, 1, c * C:(c + 1) * C], work[u][:, :],
                                  qk[:, y, 0, c * C:(c + 1) * C].bitcast(F32), ALU.subtract
                                  ).then_inc(work_free[u], 1)
            elif kind == "w":
                dve.wait_ge(w_hi, g * KC + KC + c + 1)
                dve.tensor_tensor(w[:, :, 1, c, :], work[u][:, 0:3 * P].rearrange("p (y c) -> p y c", c=P),
                                  w[:, :, 0, c, :].bitcast(F32), ALU.subtract).then_inc(work_free[u], 1)
            elif kind == "s":
                h, t, k0, nk = SCORES[c]
                if c == 0:
                    dve.wait_ge(masks_made, 7)
                    if later(i, 1):
                        dve.wait_ge(neg_max_made, i * 3)
                dve.wait_ge(work_made, pieces(i, b, n) + 1)
                dve.tensor_reduce(part_max[:, k0 // C, h, t:t + 1], work[u][:, 0:nk], AX_X, ALU.max,
                                  negate=True).then_inc(work_free[u], 1)
                if c == NSC - 1:
                    dve.wait_ge(work_free[u], in_bank(i, b, n) + 1)
                    dve.wait_ge(work_free[1 - u], in_bank(i, b, n - 1) + 1)
                    if later(i, 1):
                        dve.wait_ge(work_made, pieces(i, b, 0))
                    dve.tensor_tensor(neg_max[:, :, :], part_max[:, 0, :, :], part_max[:, 1, :, :],
                                      ALU.min).then_inc(neg_max_made, 1)
                    dve.wait_ge(neg_max_made, i * 3 + 1)
                    dve.tensor_copy(neg_max_parts[:, 0, :, :].bitcast(F32R), neg_max[:, :, :]
                                    ).then_inc(neg_max_made, 1)
                    dve.wait_ge(neg_max_made, i * 3 + 2)
                    dve.tensor_tensor(neg_max_parts[:, 1, :, :], neg_max[:, :, :],
                                      neg_max_parts[:, 0, :, :], ALU.subtract).then_inc(neg_max_made, 1)
            elif kind == "m":
                dve.wait_ge(work_made, pieces(i, b, n) + 1)
                if c == 0 and later(i, 1):
                    dve.wait_ge(max_rows_in[1 - b], (i - 1 - (1 - b)) * 16 + 32)
                dve.tensor_copy(max_rows[c * GH * QT:(c + 1) * GH * QT, :], work[u][0:GH * QT, 0:P]
                                ).then_inc(work_free[u], 1)

        def attend_slot(i, b, g, s, slot):
            def reciprocals(c, k):
                if k == 0:
                    dve.wait_ge(out_copied, (i * NC + c) * 2 + 1)
                    if later(i, 1) or c > 0:
                        dve.wait_ge(attn_made, i * NC + c)
                cols = slice(k * C // RQ, (k + 1) * C // RQ)
                dve.reciprocal(rdenom[:, cols], denom_copy[:, cols]).then_inc(rdenom_made, 1)

            if s == NS:
                for k in range(RQ):
                    reciprocals(NC - 1, k)
            elif slot in (1, 3):
                for c in range(NC - 1):
                    after = next(m for m in range(NS) if ends_chunk(m, 0) == c)
                    k = (s - after) * 2 + slot // 2
                    if 0 <= k < RQ:
                        reciprocals(c, k)

        turns(dve, prepare, attend_slot)


def feed(nc, ctx, identf, identb, feed_weights, h_dram, attnT_dram, out):
    sb, ps, sem = allocators(nc, ctx, "feed")
    wguT, wdT, srow, wo_rows = feed_weights
    woT = sb("woT", [P, KC, D])
    attn_in = sb("attn_in", [P, 2, KC, P])
    h_in = sb("h_in", [P, 2, D])
    h2 = sb("h2", [P, 2, D])
    h2_kept = sb("h2_kept", [P, 2, D])
    stats = sb("stats", [P, 2, 6])
    mean_var = sb("mean_var", [P, 2, 2])
    var_eps = sb("var_eps", [P, 2])
    rstd = sb("rstd", [P, 2])
    minus_half = sb("minus_half", [P, 1])
    eps = sb("eps", [P, 1])
    xn = sb("xn", [P, 2, D])
    x_max = sb("x_max", [P, 2])
    x_scale = sb("x_scale", [P, 2])
    x_rscale = sb("x_rscale", [P, 2])
    x_scaled = sb("x_scaled", [P, 2, D])
    x_magic = sb("x_magic", [P, 2, D], U32)
    x_rounded = sb("x_rounded", [P, 2, D], BF16)
    xT = [sb(f"xT{u}", [P, KC, P], BF16) for u in range(2)]
    gate = sb("gate", [P, 2, I_FF])
    up = sb("up", [P, 2, I_FF])
    t_max = sb("t_max", [P, 2])
    t_scale = sb("t_scale", [P, 2])
    t_rscale = sb("t_rscale", [P, 2])
    t_scaled = sb("t_scaled", [P, 2, I_FF])
    t_magic = sb("t_magic", [P, 2, I_FF], U32)
    t_rounded = sb("t_rounded", [P, 2, I_FF], BF16)
    tT = sb("tT", [P, NI, P], BF16)
    y_down = sb("y_down", [P, D])
    y = sb("y", [P, 2, D])

    proj = ps("proj", [P, D])
    down = ps("down", [P, D])
    gu = [ps(f"gu{k}", [P, D]) for k in range(4)]
    t_turned = ps("t_turned", [P, 2048], BF16)[:, 0:I_FF]
    x_turned = gu[3][:, 0:D // 2].bitcast(BF16)

    wo_turned = sem("wo_turned")
    wo_made = sem("wo_made")
    consts_made = sem("consts_made")
    attn_in_ = [sem(f"attn_in{u}") for u in range(2)]
    h_in_ = [sem(f"h_in{u}") for u in range(2)]
    proj_made = sem("proj_made")
    h2_made = sem("h2_made")
    h2_kept_made = sem("h2_kept_made")
    stats_made = sem("stats_made")
    mean_made = sem("mean_made")
    var_made = sem("var_made")
    rstd_made = sem("rstd_made")
    xn_made = sem("xn_made")
    x_max_made = sem("x_max_made")
    x_scale_made = sem("x_scale_made")
    x_rscale_made = sem("x_rscale_made")
    x_scaled_made = sem("x_scaled_made")
    x_power_made = sem("x_power_made")
    x_magic_made = sem("x_magic_made")
    x_sum_made = sem("x_sum_made")
    x_rounded_made = sem("x_rounded_made")
    x_turned_made = sem("x_turned_made")
    xT_made = sem("xT_made")
    gu_made = sem("gu_made")
    gu_used = sem("gu_used")
    silu_made = sem("silu_made")
    t_made = sem("t_made")
    t_max_made = sem("t_max_made")
    t_scale_made = sem("t_scale_made")
    t_rscale_made = sem("t_rscale_made")
    t_scaled_made = sem("t_scaled_made")
    t_power_made = sem("t_power_made")
    t_magic_made = sem("t_magic_made")
    t_sum_made = sem("t_sum_made")
    t_rounded_made = sem("t_rounded_made")
    t_turned_made = sem("t_turned_made")
    tT_made = sem("tT_made")
    down_made = sem("down_made")
    y_down_made = sem("y_down_made")
    y_rescaled = sem("y_rescaled")
    y_made = sem("y_made")
    y_stored = [sem(f"y_stored{u}") for u in range(2)]

    out_rows = out.rearrange("b s d -> (b s) d")
    block = ctx.enter_context(nc.Block())

    def turns(eng, turn):
        turn(-3, 1, "A")
        turn(-2, 0, "AB")
        turn(-1, 1, "ABM")
        for n in range(2):
            turn(n, n, "ABMC")
        with eng.Fori(1, NT // 2 - 2) as t:
            for u in range(2):
                turn(t * 2 + u, u, "ABMC")
        turn(NT - 4, 0, "ABMC")
        turn(NT - 3, 1, "BMC")
        turn(NT - 2, 0, "MC")
        turn(NT - 1, 1, "C")

    def loaded(n, u):
        return (n - u) * 8 + 16

    def wo_bank(r):
        return gu[r][:, :].rearrange("p (k c) -> p k c", c=P)

    @block.sync
    def _(sp):
        def load(n, u):
            if later(n, 2):
                sp.wait_ge(proj_made, n - 1)
            sp.dma_start(attn_in[:, u, :, :],
                         attnT_dram[:, :, ds(n * P, P)].rearrange("g p n -> p g n")
                         ).then_inc(attn_in_[u], 16)
            if later(n, 2):
                sp.wait_ge(proj_made, n - 1)
            sp.dma_start(h_in[:, u, :], h_dram[ds(n, 1), :, :].rearrange("a p n -> p (a n)")
                         ).then_inc(h_in_[u], 16)

        def turn(n, u, stages):
            if not isinstance(n, int) or -2 <= n < NT - 4:
                load(n + 4, u)
            if "C" in stages:
                sp.wait_ge(y_made, n + 1)
                sp.dma_start(out_rows[ds(n * P, P), :], y[:, u, :]).then_inc(y_stored[u], 16)

        load(0, 0)
        load(1, 1)
        turns(sp, turn)
        for u in range(2):
            sp.wait_ge(y_stored[u], 16 * NT // 2)

    @block.gpsimd
    def _(pool):
        def turn(n, u, stages):
            v = 1 - u
            if "A" in stages:
                m = n + 3
                pool.wait_ge(mean_made, m + 1)
                pool.tensor_tensor(var_eps[:, v:v + 1], mean_var[:, v, 1:2], eps[:, :], ALU.add
                                   ).then_inc(var_made, 1)
                pool.wait_ge(var_made, m + 1)
                pool.tensor_tensor(rstd[:, v:v + 1], var_eps[:, v:v + 1], minus_half[:, :], ALU.pow
                                   ).then_inc(rstd_made, 1)
            if "M" in stages:
                m = n + 1
                pool.wait_ge(t_magic_made, m + 1)
                pool.tensor_tensor(t_scaled[:, v, :], t_scaled[:, v, :], t_magic[:, v, :].bitcast(F32),
                                   ALU.add).then_inc(t_sum_made, 1)
            if "C" in stages:
                pool.wait_ge(y_down_made, n + 1)
                pool.tensor_tensor(y_down[:, :], y_down[:, :], srow[:, 0:D], ALU.mult
                                   ).then_inc(y_rescaled, 1)
                pool.wait_ge(y_rescaled, n + 1)
                pool.wait_ge(h2_kept_made, n + 1)
                if later(n, 2):
                    pool.wait_ge(y_stored[u], (n - u) * 8)
                pool.tensor_tensor(y[:, u, :], y_down[:, :],
                                   h2_kept[:, u, :], ALU.add).then_inc(y_made, 1)
            if "M" in stages:
                m = n + 1
                pool.wait_ge(t_sum_made, m + 1)
                if later(m, 2):
                    pool.wait_ge(t_turned_made, m - 1)
                pool.tensor_tensor(t_rounded[:, v, :], t_scaled[:, v, :], t_magic[:, v, :].bitcast(F32),
                                   ALU.subtract).then_inc(t_rounded_made, 1)
            if "A" in stages:
                m = n + 3
                pool.wait_ge(x_magic_made, m + 1)
                pool.tensor_tensor(x_scaled[:, v, :], x_scaled[:, v, :],
                                   x_magic[:, v, :].bitcast(F32), ALU.add).then_inc(x_sum_made, 1)
                pool.wait_ge(x_sum_made, m + 1)
                if later(m, 2):
                    pool.wait_ge(x_turned_made, m - 1)
                pool.tensor_tensor(x_rounded[:, v, :], x_scaled[:, v, :],
                                   x_magic[:, v, :].bitcast(F32), ALU.subtract
                                   ).then_inc(x_rounded_made, 1)

        pool.memset(minus_half[:, :], -0.5).then_inc(consts_made, 1)
        pool.memset(eps[:, :], EPS).then_inc(consts_made, 1)
        pool.wait_ge(consts_made, 2)
        turns(pool, turn)

    @block.scalar
    def _(act):
        def turn(n, u, stages):
            v = 1 - u

            def silu(half):
                m = n + 2
                act.wait_ge(gu_used, m * NGC + 2 * half + 2)
                cols = slice(half * 2 * GC, (half + 1) * 2 * GC)
                act.activation(gate[:, u, cols], gate[:, u, cols], ACT.Silu).then_inc(silu_made, 1)

            if "C" in stages:
                act.wait_ge(t_turned_made, n + 1)
                if later(n, 1):
                    act.wait_ge(down_made, n)
                act.activation(tT[:, :, :], t_turned.rearrange("p (k c) -> p k c", c=P),
                               ACT.Copy).then_inc(tT_made, 1)
            if "M" in stages:
                m = n + 1
                act.wait_ge(t_rscale_made, m + 1)
                if later(m, 2):
                    act.wait_ge(t_rounded_made, m - 1)
                act.activation(t_scaled[:, v, :], up[:, v, :], ACT.Copy, scale=t_rscale[:, v:v + 1]
                               ).then_inc(t_scaled_made, 1)
            if "B" in stages:
                m = n + 2
                act.wait_ge(x_turned_made, m + 1)
                if later(m, 2):
                    act.wait_ge(gu_made, (m - 1) * NGC)
                act.activation(xT[u][:, :, :], x_turned.rearrange("p (k c) -> p k c", c=P),
                               ACT.Copy).then_inc(xT_made, 1)
            if "A" in stages:
                m = n + 3
                act.wait_ge(stats_made, m + 1)
                if later(m, 2):
                    act.wait_ge(h2_kept_made, m - 1)
                act.activation(h2[:, v, :], proj[:, :], ACT.Copy).then_inc(h2_made, 1)
            if "A" in stages:
                m = n + 3
                act.wait_ge(x_rscale_made, m + 1)
                if later(m, 2):
                    act.wait_ge(x_rounded_made, m - 1)
                act.activation(x_scaled[:, v, :], xn[:, v, :], ACT.Copy, scale=x_rscale[:, v:v + 1]
                               ).then_inc(x_scaled_made, 1)
            if "C" in stages:
                act.wait_ge(down_made, n + 1)
                if later(n, 1):
                    act.wait_ge(y_made, n)
                act.activation(y_down[:, :], down[:, :], ACT.Copy, scale=t_scale[:, u:u + 1]
                               ).then_inc(y_down_made, 1)
            if "B" in stages:
                silu(0)
            if "B" in stages:
                m = n + 2
                act.wait_ge(h2_made, m + 1)
                if later(m, 2):
                    act.wait_ge(y_made, m - 1)
                act.activation(h2_kept[:, u, :], h2[:, u, :], ACT.Copy).then_inc(h2_kept_made, 1)
                silu(1)

        for r in range(KC):
            act.wait_ge(wo_turned, r + 1)
            act.activation(woT[:, :, r * P:(r + 1) * P], wo_bank(r), ACT.Copy).then_inc(wo_made, 1)
        turns(act, turn)

    @block.vector
    def _(dve):
        def turn(n, u, stages):
            v = 1 - u
            a, b, m_, c = (stage in stages for stage in "ABMC")

            def gate_up(k):
                m = n + 2
                if k == 0 and later(m, 2):
                    dve.wait_ge(t_scaled_made, m - 1)
                dve.wait_ge(gu_made, m * NGC + k + 1)
                cols = slice(k * GC, (k + 1) * GC)
                for y_, to in enumerate((gate, up)):
                    col = D + y_ * I_FF + k * GC
                    last = dve.scalar_tensor_tensor(
                        out=to[:, u, cols], in0=gu[2 * (k % 2) + y_][:, 0:GC],
                        scalar=x_scale[:, u:u + 1], in1=srow[:, col:col + GC],
                        op0=ALU.mult, op1=ALU.mult)
                last.then_inc(gu_used, 1)

            if a:
                m = n + 3
                dve.wait_ge(proj_made, m + 1)
                dve.bn_stats(stats[:, v, :], proj[:, :]).then_inc(stats_made, 1)
                dve.wait_ge(stats_made, m + 1)
            if m_:
                dve.wait_ge(t_scaled_made, n + 2)
                if later(n + 1, 2):
                    dve.wait_ge(t_rounded_made, n)
                dve.tensor_scalar(t_magic[:, v, :], t_scaled[:, v, :].bitcast(U32), 0x7F800000, None,
                                  ALU.bitwise_and).then_inc(t_power_made, 1)
            if a:
                if not m_:
                    dve.tensor_copy(x_max[:, v:v + 1], stats[:, v, 0:1]).then_inc(x_max_made, 1)
                dve.bn_aggr(mean_var[:, v, :], stats[:, v, :]).then_inc(mean_made, 1)
            if m_:
                dve.wait_ge(t_power_made, n + 2)
                dve.tensor_scalar(t_magic[:, v, :].bitcast(F32), t_magic[:, v, :].bitcast(F32),
                                  NORMAL_MIN, 1.5 * SHIFT, ALU.max, ALU.mult).then_inc(t_magic_made, 1)
            if a:
                dve.wait_ge(rstd_made, m + 1)
                if later(m, 2):
                    dve.wait_ge(x_scaled_made, m - 1)
                dve.wait_ge(h2_made, m + 1)
                dve.tensor_scalar(xn[:, v, :], h2[:, v, :], mean_var[:, v, 0:1], rstd[:, v:v + 1],
                                  ALU.subtract, ALU.mult).then_inc(xn_made, 1)
                dve.wait_ge(xn_made, m + 1)
                dve.tensor_reduce(x_max[:, v:v + 1], xn[:, v, :], AX_X, ALU.max,
                                  apply_absolute_value=True).then_inc(x_max_made, 1)
                dve.wait_ge(x_max_made, m + 1 + (min(m, 1) + 1 if isinstance(m, int) else 2))
                dve.tensor_scalar(x_scale[:, v:v + 1], x_max[:, v:v + 1], 1.0 / FP8_MAX, None,
                                  ALU.mult).then_inc(x_scale_made, 1)
                dve.wait_ge(x_scale_made, m + 1)
                dve.reciprocal(x_rscale[:, v:v + 1], x_scale[:, v:v + 1]).then_inc(x_rscale_made, 1)
            if b:
                gate_up(0)
                gate_up(1)
            if a:
                dve.wait_ge(x_scaled_made, m + 1)
                if later(m, 2):
                    dve.wait_ge(x_rounded_made, m - 1)
                dve.tensor_scalar(x_magic[:, v, :], x_scaled[:, v, :].bitcast(U32), 0x7F800000, None,
                                  ALU.bitwise_and).then_inc(x_power_made, 1)
                dve.wait_ge(x_power_made, m + 1)
                dve.tensor_scalar(x_magic[:, v, :].bitcast(F32), x_magic[:, v, :].bitcast(F32),
                                  NORMAL_MIN, 1.5 * SHIFT, ALU.max, ALU.mult).then_inc(x_magic_made, 1)
            if b:
                gate_up(2)
                gate_up(3)
                m = n + 2
                for half in range(2):
                    dve.wait_ge(silu_made, m * 2 + half + 1)
                    cols = slice(half * 2 * GC, (half + 1) * 2 * GC)
                    dve.tensor_tensor(up[:, u, cols], gate[:, u, cols], up[:, u, cols], ALU.mult
                                      ).then_inc(t_made, 1)
                dve.wait_ge(t_made, m * 2 + 2)
                dve.tensor_reduce(t_max[:, u:u + 1], up[:, u, :], AX_X, ALU.max,
                                  apply_absolute_value=True).then_inc(t_max_made, 1)
                if later(m, 2):
                    dve.wait_ge(y_down_made, m - 1)
                dve.wait_ge(t_max_made, m + 1)
                dve.tensor_scalar(t_scale[:, u:u + 1], t_max[:, u:u + 1], 1.0 / FP8_MAX, None,
                                  ALU.mult).then_inc(t_scale_made, 1)
                dve.wait_ge(t_scale_made, m + 1)
                dve.reciprocal(t_rscale[:, u:u + 1], t_scale[:, u:u + 1]).then_inc(t_rscale_made, 1)

        turns(dve, turn)

    @block.tensor
    def _(pe):
        def turn(n, u, stages):
            v = 1 - u

            def products(chunks):
                m = n + 2
                for k in chunks:
                    if later(m, 1) or k >= 2:
                        pe.wait_ge(gu_used, m * NGC + k - 1)
                    for y_, col in ((0, 0), (1, I_FF)):
                        for kc in range(KC):
                            mm = pe.matmul(gu[2 * (k % 2) + y_][:, 0:GC], xT[u][:, kc, :],
                                           wguT[:, kc, col + k * GC:col + (k + 1) * GC],
                                           start=(kc == 0), stop=(kc == KC - 1))
                    mm.then_inc(gu_made, 1)

            if "A" in stages:
                m = n + 3
                pe.wait_ge(attn_in_[v], loaded(m, v))
                pe.wait_ge(h_in_[v], loaded(m, v))
                if later(m, 1):
                    pe.wait_ge(h2_made, m)
                for k in range(KC):
                    pe.matmul(proj[:, :], attn_in[:, v, k, :], woT[:, k, :], start=(k == 0), stop=False)
                pe.matmul(proj[:, :], identf[:, :], h_in[:, v, :], start=False, stop=True
                          ).then_inc(proj_made, 1)
            if "C" in stages:
                pe.wait_ge(t_rounded_made, n + 1)
                if later(n, 1):
                    pe.wait_ge(tT_made, n)
                for k in range(NI):
                    mm = pe.transpose(t_turned[:, k * P:(k + 1) * P], t_rounded[:, u, k * P:(k + 1) * P],
                                      identb[:, :])
                mm.then_inc(t_turned_made, 1)
            if "B" in stages:
                m = n + 2
                pe.wait_ge(x_rounded_made, m + 1)
                if later(m, 1):
                    pe.wait_ge(gu_used, m * NGC)
                for k in range(KC):
                    mm = pe.transpose(x_turned[:, k * P:(k + 1) * P], x_rounded[:, u, k * P:(k + 1) * P],
                                      identb[:, :])
                mm.then_inc(x_turned_made, 1)
            if "C" in stages:
                pe.wait_ge(tT_made, n + 1)
                if later(n, 1):
                    pe.wait_ge(y_down_made, n)
                for k in range(NI):
                    mm = pe.matmul(down[:, :], tT[:, k, :], wdT[:, k, :], start=(k == 0),
                                   stop=(k == NI - 1))
                mm.then_inc(down_made, 1)
            if "B" in stages:
                m = n + 2
                pe.wait_ge(xT_made, m + 1)
                products(range(NGC))

        for r in range(KC):
            for k in range(KC):
                mm = pe.transpose(wo_bank(r)[:, k, :], wo_rows[:, r, k * P:(k + 1) * P], identf[:, :])
            mm.then_inc(wo_turned, 1)
        pe.wait_ge(wo_made, KC)
        turns(pe, turn)


_INS = ["x", "L0_tok_weight", "L0_tok_lora_A", "L0_tok_lora_B", "L0_attn_W_qkv", "L0_attn_W_out",
        "L0_ffn_w_gate", "L0_ffn_w_up", "L0_ffn_w_down", "L0_ffn_up_reorder_index",
        "L0_ffn_down_reorder_index"]


def kernel(**inputs):
    import numpy as _np
    import concourse.bacc as _bacc
    from concourse import mybir as _mybir
    from concourse.bass_utils import run_bass_kernel_spmd as _run

    nc = _bacc.Bacc("TRN2", target_bir_lowering=False, num_devices=1)
    arrays, args = {}, []
    for name in _INS:
        a = _np.ascontiguousarray(inputs[name])
        arrays[f"in_{name}_dram"] = a
        args.append(nc.dram_tensor(f"in_{name}_dram", a.shape, _mybir.dt.from_np(a.dtype),
                                   kind="ExternalInput").ap())
    out = nc.dram_tensor("out_dram", (B, S, D), _mybir.dt.float32, kind="ExternalOutput").ap()
    build(nc, *args, out)
    r = _run(nc, [arrays], core_ids=[0])
    return r.results[0]["out_dram"]
```
